# Optimizing a Trainium2 kernel written in Bass

```python
import numpy as np
import jax
import jax.numpy as jnp

def _softmax(x, axis=-1):
    return jax.nn.softmax(x, axis=axis)

def _gelu(x):
    return jax.nn.gelu(x, approximate=True)

def _silu(x):
    return jax.nn.silu(x)

def _sigmoid(x):
    return jax.nn.sigmoid(x)

def _layernorm(x, axis=-1, eps=1e-05):
    m = jnp.mean(x, axis=axis, keepdims=True)
    v = jnp.var(x, axis=axis, keepdims=True)
    return (x - m) / jnp.sqrt(v + eps)

def _scatter_add(tgt, idx, src, axis=0):
    return tgt.at[idx].add(src)

def _segment_sum(src, seg, n):
    return jax.ops.segment_sum(src, seg, n)
kernel_name = 'mk_adj_resnorm_d4_adj_r2_ec2223'

def setup_inputs(seed: int=0):
    np.random.seed(seed)
    _w = jnp.asarray

    def _rec_inputs():
        import jax
        import jax.numpy as jnp
        _gk = jax.random.key(seed)
        x = -0.0002928 + 1 * jax.random.normal(jax.random.fold_in(_gk, 1), (3327, 256), jnp.float32)
        _a = jax.random.bernoulli(jax.random.fold_in(_gk, 2), 0.00480914, (3327, 3327))
        _af = _a.astype(jnp.float32)
        adj = _af
        return (x, adj)
    x, adj = _rec_inputs()

    def _L0_gnn_setup():
        import jax, jax.numpy as jnp
        import numpy as np
        N = 4096
        D_IN = 256
        HEADS = 8
        DPH = 256 // HEADS
        EDGE_P = 0.01
        key = jax.random.key(seed)
        k1, k2, k3 = jax.random.split(key, 3)
        H = jax.random.normal(k1, (N, D_IN), dtype=jnp.float32)
        adj = (jax.random.uniform(k2, (N, N)) < EDGE_P).astype(jnp.float32)
        limit = float(np.sqrt(6.0 / (D_IN + DPH)))
        W = jax.random.uniform(k3, (HEADS, D_IN, DPH), jnp.float32, -limit, limit)
        b = jnp.zeros((HEADS, DPH), jnp.float32)
        return {'H': H, 'adj': adj, 'W': W, 'b': b}
    _L0_gnn_all = _L0_gnn_setup()
    _L0_gnn_in = {k: v for k, v in _L0_gnn_all.items() if k in ('W', 'b')}
    del _L0_gnn_all

    def _L1_gnn_setup():
        import jax, jax.numpy as jnp
        import numpy as np
        N = 3072
        D_IN = 256
        D_OUT = 256
        DENSITY = 0.005
        key = jax.random.key(seed)
        ks = jax.random.split(key, 12)
        x = jax.random.normal(ks[0], (N, D_IN), dtype=jnp.float32)
        adj_a = (jax.random.uniform(ks[1], (N, N)) < DENSITY).astype(jnp.float32)
        adj_b = (jax.random.uniform(ks[2], (N, N)) < DENSITY).astype(jnp.float32)
        W_sa = jax.random.normal(ks[3], (D_IN, D_OUT), dtype=jnp.float32) * (1.414 / np.sqrt(D_IN + D_OUT))
        a_sa = jax.random.normal(ks[4], (1, 2 * D_OUT), dtype=jnp.float32) * (1.414 / np.sqrt(1 + 2 * D_OUT))
        stdv = 1.0 / np.sqrt(D_OUT)
        W_gcnb = jax.random.uniform(ks[5], (D_IN, D_OUT), minval=-stdv, maxval=stdv, dtype=jnp.float32)
        b_gcnb = jax.random.uniform(ks[6], (D_OUT,), minval=-stdv, maxval=stdv, dtype=jnp.float32)
        s = 1.0 / np.sqrt(2 * D_IN)
        Wa = jax.random.uniform(ks[7], (1, 2 * D_IN), minval=-s, maxval=s, dtype=jnp.float32)
        ba = jax.random.uniform(ks[8], (1,), minval=-s, maxval=s, dtype=jnp.float32)
        Wb = jax.random.uniform(ks[9], (1, 2 * D_IN), minval=-s, maxval=s, dtype=jnp.float32)
        bb = jax.random.uniform(ks[10], (1,), minval=-s, maxval=s, dtype=jnp.float32)
        return {'x': x, 'adj_a': adj_a, 'adj_b': adj_b, 'W_sa': W_sa, 'a_sa': a_sa, 'W_gcnb': W_gcnb, 'b_gcnb': b_gcnb, 'Wa': Wa, 'ba': ba, 'Wb': Wb, 'bb': bb}
    _L1_gnn_all = _L1_gnn_setup()
    _L1_gnn_in = {k: v for k, v in _L1_gnn_all.items() if k in ('W_sa', 'a_sa', 'W_gcnb', 'b_gcnb', 'Wa', 'ba', 'Wb', 'bb')}
    del _L1_gnn_all

    def _L2_gnn_setup():
        import jax, jax.numpy as jnp
        import numpy as np
        N = 4096
        F_IN = 256
        F_OUT = 256
        DENSITY = 0.01
        key = jax.random.key(seed)
        k_x, k_adj, k_w, k_b = jax.random.split(key, 4)
        input_features = jax.random.normal(k_x, (N, F_IN), dtype=jnp.float32)
        adj = (jax.random.uniform(k_adj, (N, N)) < DENSITY).astype(jnp.float32)
        idx = jnp.arange(N)
        adj = adj.at[idx, idx].set(1.0)
        W = jax.random.normal(k_w, (F_IN, F_OUT), dtype=jnp.float32) / np.sqrt(F_IN)
        b = jax.random.normal(k_b, (F_OUT,), dtype=jnp.float32) * 0.01
        return {'input_features': input_features, 'adj': adj, 'W': W, 'b': b}
    _L2_gnn_all = _L2_gnn_setup()
    _L2_gnn_in = {k: v for k, v in _L2_gnn_all.items() if k in ('W', 'b')}
    del _L2_gnn_all

    def _L3_gnn_setup():
        import jax, jax.numpy as jnp
        import numpy as np
        N, IN_F, OUT_F = (4096, 256, 256)
        HID = OUT_F // 2
        key = jax.random.key(seed)
        ks = jax.random.split(key, 6)
        x = jax.random.normal(ks[0], (N, IN_F), dtype=jnp.float32)
        adj = jax.random.uniform(ks[1], (N, N), dtype=jnp.float32)
        W1 = jax.random.normal(ks[2], (HID, IN_F), dtype=jnp.float32) * np.sqrt(2.0 / IN_F)
        b1 = jnp.zeros((HID,), dtype=jnp.float32)
        W2 = jax.random.normal(ks[3], (OUT_F, HID), dtype=jnp.float32) * np.sqrt(2.0 / HID)
        b2 = jnp.zeros((OUT_F,), dtype=jnp.float32)
        return {'x': x, 'adj': adj, 'W1': W1, 'b1': b1, 'W2': W2, 'b2': b2}
    _L3_gnn_all = _L3_gnn_setup()
    _L3_gnn_in = {k: v for k, v in _L3_gnn_all.items() if k in ('W1', 'b1', 'W2', 'b2')}
    del _L3_gnn_all
    return {'x': x, 'adj': adj, 'L0_gnn_W': _L0_gnn_in['W'], 'L0_gnn_b': _L0_gnn_in['b'], 'L1_gnn_W_sa': _L1_gnn_in['W_sa'], 'L1_gnn_a_sa': _L1_gnn_in['a_sa'], 'L1_gnn_W_gcnb': _L1_gnn_in['W_gcnb'], 'L1_gnn_b_gcnb': _L1_gnn_in['b_gcnb'], 'L1_gnn_Wa': _L1_gnn_in['Wa'], 'L1_gnn_ba': _L1_gnn_in['ba'], 'L1_gnn_Wb': _L1_gnn_in['Wb'], 'L1_gnn_bb': _L1_gnn_in['bb'], 'L2_gnn_W': _L2_gnn_in['W'], 'L2_gnn_b': _L2_gnn_in['b'], 'L3_gnn_W1': _L3_gnn_in['W1'], 'L3_gnn_b1': _L3_gnn_in['b1'], 'L3_gnn_W2': _L3_gnn_in['W2'], 'L3_gnn_b2': _L3_gnn_in['b2']}

def reference(x, adj, L0_gnn_W, L0_gnn_b, L1_gnn_W_sa, L1_gnn_a_sa, L1_gnn_W_gcnb, L1_gnn_b_gcnb, L1_gnn_Wa, L1_gnn_ba, L1_gnn_Wb, L1_gnn_bb, L2_gnn_W, L2_gnn_b, L3_gnn_W1, L3_gnn_b1, L3_gnn_W2, L3_gnn_b2):
    import jax
    import jax.numpy as jnp

    def _L0_gnn_ref(H, adj, W, b):
        import jax, jax.numpy as jnp
        import numpy as np
        N = 4096
        D_IN = 256
        HEADS = 8
        DPH = 256 // HEADS
        EDGE_P = 0.01
        H_ = jnp.einsum('nd,hde->hne', H, W)
        out = jnp.einsum('nm,hme->hne', adj, H_) + b[:, None, :]
        return jnp.transpose(out, (1, 0, 2)).reshape(H.shape[0], HEADS * DPH)

    def _L1_gnn_ref(x, adj_a, adj_b, W_sa, a_sa, W_gcnb, b_gcnb, Wa, ba, Wb, bb):
        import jax, jax.numpy as jnp
        import numpy as np
        N = 3072
        D_IN = 256
        D_OUT = 256
        DENSITY = 0.005
        type_sum_a = adj_a @ x
        type_sum_b = adj_b @ x
        attn_a = jax.nn.sigmoid(jnp.concatenate([type_sum_a, x], axis=1) @ Wa.T + ba)
        attn_b = jax.nn.sigmoid(jnp.concatenate([type_sum_b, x], axis=1) @ Wb.T + bb)
        h = x @ W_sa
        Hd = h.shape[1]
        s_left = h @ a_sa[0, :Hd]
        s_right = h @ a_sa[0, Hd:]
        scores = s_left[:, None] + s_right[None, :]
        e = jnp.where(adj_a != 0, jnp.exp(-jax.nn.leaky_relu(scores, 0.01)), 0.0)
        attn = e / (jnp.sum(e, axis=1, keepdims=True) + 1e-05)
        x_a = attn @ h
        x_b = adj_b @ (x @ W_gcnb) + b_gcnb
        return jax.nn.sigmoid(attn_a * x_a + attn_b * x_b)

    def _L2_gnn_ref(input_features, adj, W, b):
        import jax, jax.numpy as jnp
        import numpy as np
        N = 4096
        F_IN = 256
        F_OUT = 256
        DENSITY = 0.01
        A = (adj != 0).astype(input_features.dtype)
        hidden = input_features @ W + b
        deg = jnp.sum(A, axis=0)
        return A @ hidden / deg[:, None]

    def _L3_gnn_ref(x, adj, W1, b1, W2, b2):
        import jax, jax.numpy as jnp
        import numpy as np
        N, IN_F, OUT_F = (4096, 256, 256)
        HID = OUT_F // 2
        h = x @ W1.T + b1
        h = h @ W2.T + b2
        A = adj + jnp.eye(adj.shape[0], dtype=adj.dtype)
        rowsum = A.sum(axis=1)
        r_inv_sqrt = jnp.power(rowsum, -0.5)
        r_inv_sqrt = jnp.where(jnp.isinf(r_inv_sqrt), 0.0, r_inv_sqrt)
        A = r_inv_sqrt[:, None] * A * r_inv_sqrt[None, :]
        return A.astype(jnp.float32) @ h.astype(jnp.float32)
    x = _layernorm(x + _L0_gnn_ref(x, adj, L0_gnn_W, L0_gnn_b), axis=-1)
    x = _layernorm(x + _L1_gnn_ref(x, adj, adj, L1_gnn_W_sa, L1_gnn_a_sa, L1_gnn_W_gcnb, L1_gnn_b_gcnb, L1_gnn_Wa, L1_gnn_ba, L1_gnn_Wb, L1_gnn_bb), axis=-1)
    x = _layernorm(x + _L2_gnn_ref(x, adj, L2_gnn_W, L2_gnn_b), axis=-1)
    x = _layernorm(x + _L3_gnn_ref(x, adj, L3_gnn_W1, L3_gnn_b1, L3_gnn_W2, L3_gnn_b2), axis=-1)
    return x

_drawn_inputs = setup_inputs


def setup_inputs(seed=0):
    import zlib

    import numpy as np

    out = dict(_drawn_inputs(seed))
    spreads = {'L0_gnn_b': (0.0, 0.1), 'L3_gnn_b1': (0.0, 0.1), 'L3_gnn_b2': (0.0, 0.1)}
    factors = {'L1_gnn_a_sa': 3.586, 'L1_gnn_b_gcnb': 6.831, 'L1_gnn_Wa': 3.363, 'L2_gnn_b': 3.285}
    for name, (base, spread) in spreads.items():
        noise = np.random.default_rng([zlib.crc32(name.encode()), seed]).standard_normal(out[name].shape)
        drawn = base * np.exp(spread * noise) if base else spread * noise
        out[name] = jnp.asarray(drawn.astype(out[name].dtype))
    for name, factor in factors.items():
        out[name] = (out[name] * factor).astype(out[name].dtype)
    return out
```

```python
import concourse.bass as bass
from concourse import mybir
from contextlib import ExitStack


def four_graph_layers(nc, x, adj, w0, b0, w_sa, a_sa, w_gcn, b_gcn, wa, ba, wb, bb, w2, b2,
                      w31, b31, w32, b32, out):
    F32, BF16, F16 = mybir.dt.float32, mybir.dt.bfloat16, mybir.dt.float16
    U8, I32 = mybir.dt.uint8, mybir.dt.int32
    ALU, ACT, AX = mybir.AluOpType, mybir.ActivationFunctionType, mybir.AxisListType

    P = 128
    N, D = x.shape
    NB = (N + P - 1) // P
    NP = NB * P
    TAIL = N - (NB - 1) * P
    TAIL_A = TAIL // 16 * 16
    Q = NB // 2
    PAIRS = (Q - 1) // 2
    WIDE, NARROW = 512, 256
    CH = NP // WIDE + 1
    HALVES = NP // NARROW
    HEADS, DPH = w0.shape[0], w0.shape[2]
    EPS = 1e-5
    XS = 2.0 ** 11
    US = 2.0 ** 10
    EXPONENT = 0x7F800000
    assert D == 2 * P and NB % 2 == 0 and PAIRS == 6 and (CH - 1) * WIDE + NARROW == NP

    SW1 = HALVES
    SW2 = SW1 + 3 * CH
    SW3 = SW2 + CH
    ZT1 = HALVES
    ZT2 = ZT1 + CH
    ZT3 = ZT2 + CH

    ctx = ExitStack()
    with ctx:
        def sb(name, shape, dt):
            return ctx.enter_context(nc.sbuf_tensor(name, shape, dt))

        def sem(name):
            return ctx.enter_context(nc.semaphore(name))

        adj_t = sb("adj_t", [P, NB, NP], U8)
        x32 = sb("x32", [P, NB, D], F32)
        xs = sb("xs", [P, NB, 2, D], F16)
        zone = sb("zone", [P, 2 * NP * 2 * 2], BF16)
        raw = zone[:, 0:4 * NP].bitcast(F32).rearrange("p (s n) -> p s n", s=2)
        rawb = zone[:, 4 * NP:8 * NP].rearrange("p (s n) -> p s n", s=4)
        ds = zone[:, 0:4 * NP].bitcast(F16).rearrange("p (m t d) -> p m t d", m=NB, t=2)
        bs = zone[:, 4 * NP:8 * NP].bitcast(F16).rearrange("p (m t d) -> p m t d", m=NB, t=2)
        w02 = sb("w02", [P, 2, D], F32)
        wg = sb("wg", [P, 2, D], F32)
        wgate = sb("wgate", [P, 2, 2], F32)
        wsa = sb("wsa", [P, 2, D], F32)
        w3 = sb("w3", [P, 2, D], F32)
        bias02 = sb("bias02", [P, D], F32)
        biasg = sb("biasg", [P, D], F32)
        bias3 = sb("bias3", [P, D], F32)
        vrow = sb("vrow", [P, 2, D], F32)
        idf = sb("idf", [P, P], F32)
        idb = sb("idb", [P, P], BF16)
        ones = sb("ones", [P, P], F32)
        onesb = sb("onesb", [P, 1], BF16)
        mhalf = sb("mhalf", [P, NB], F32)
        pad = sb("pad", [P, NB], F32)
        zt = sb("zt", [P, 2, WIDE], F32)
        ut = sb("ut", [P, 2, WIDE], F32)
        slb = sb("slb", [P, WIDE], F32)
        ring = sb("ring", [P, 2, 2, WIDE], BF16)
        m1u = sb("m1u", [P, 2, 2, WIDE], U8)
        t = sb("t", [P, 2, D], F32)
        columns = sb("columns", [P, 13, NB], F32)
        (rowsum, slc, nsr, dcol, bcol, q2, ccol, rcol, degb, r3, r3x, r3b, qcol) = (columns[:, i, :] for i in range(13))
        sxcol, onecol = ccol, rcol
        halfparts = sb("halfparts", [P, 3, NB, 2], F16)
        dpart, bpart, rpart = (halfparts[:, i, :, :] for i in range(3))
        little = sb("little", [P, 120], F32)
        taken = [0]

        def piece(*shape):
            size = 1
            for s in shape:
                size *= s
            taken[0] += size
            ap = little[:, taken[0] - size:taken[0]]
            return ap if len(shape) == 1 else ap.rearrange("p (a b) -> p a b", a=shape[0])
        vcol, kcol, mxc, bab, b31c = piece(4), piece(4), piece(4), piece(2), piece(1)
        st, mv, ve, rstd = piece(2, 6), piece(2, 2), piece(2), piece(2)
        sm, dsum, den, qs_sb = piece(24), piece(8), piece(4), piece(8)
        xab, gate, coef = piece(4, 2), piece(4, 2), piece(4, 2)
        half, eps = piece(1), piece(2)

        pairs = [ctx.enter_context(nc.psum_tensor(f"sum{i}", [P, 2, WIDE], F32)) for i in range(3)]
        prod = ctx.enter_context(nc.psum_tensor("prod", [P, WIDE], F32))
        small = ctx.enter_context(nc.psum_tensor("small", [P, WIDE], F32))
        turned = pairs[2][:, :, :].bitcast(BF16)
        PZ, PU2, PU1 = pairs[1], pairs[2], pairs[0]
        prodv = prod[:, :].rearrange("p (b d) -> p b d", b=2)

        t_asa = zt[:, 0, :]
        t_diag = ut[:, 0, :]
        t_w31 = ut[:, 1, 0:D]
        t_w32 = ut[:, 1, D:2 * D].rearrange("p (k h) -> p k h", k=2)
        t_w32t = slb[:, 0:D]
        t_b31 = slb[:, D:D + P]

        x_loaded, w_loaded, w2_loaded, wx_loaded = sem("x_loaded"), sem("w_loaded"), sem("w2_loaded"), sem("wx_loaded")
        raw_loaded = [sem("raw_loaded0"), sem("raw_loaded1")]
        out_stored = sem("out_stored")
        const_made = sem("const_made")
        prep_dve, prep_pe, prep_read, prep_pool = sem("prep_dve"), sem("prep_pe"), sem("prep_read"), sem("prep_pool")
        cast_done, quad_done, adj_kept = sem("cast_done"), sem("quad_done"), sem("adj_kept")
        tile0, tile_z, tile_u2, tile_u1 = sem("tile0"), sem("tile_z"), sem("tile_u2"), sem("tile_u1")
        step_done = sem("step_done")
        zt_ready, u2_ready, ut_ready = sem("zt_ready"), sem("u2_ready"), sem("ut_ready")
        prod_done, aff_done, y_done, st_done, mv_done = (sem("prod_done"), sem("aff_done"), sem("y_done"),
                                                         sem("st_done"), sem("mv_done"))
        ve_done, rstd_done, x_done = sem("ve_done"), sem("rstd_done"), sem("x_done")
        dot_done = sem("dot_done")
        hi_done, xs_ready = sem("hi_done"), sem("xs_ready")
        dhi_done, ds_ready, bhi_done, bs_ready = sem("dhi_done"), sem("ds_ready"), sem("bhi_done"), sem("bs_ready")
        deg_read, cols_dve, cols_act, cols_pool = sem("deg_read"), sem("cols_dve"), sem("cols_act"), sem("cols_pool")
        diag_made, slb_spread, slb_ready = sem("diag_made"), sem("slb_spread"), sem("slb_ready")
        m1u_made, rrow_made, ru_done = sem("m1u_made"), sem("rrow_made"), sem("ru_done")
        gates_done, small_read, gate_pre, gate_tanh, chunk_cols = (sem("gates_done"), sem("small_read"), sem("gate_pre"),
                                                                   sem("gate_tanh"), sem("chunk_cols"))
        p1a, p1b, p1c, th_done, sg_done = sem("p1a"), sem("p1b"), sem("p1c"), sem("th_done"), sem("sg_done")
        q_read, q_col = sem("q_read"), sem("q_col")

        waits_apart, xab_dots = sem("waits_apart"), sem("xab_dots")

        block = ctx.enter_context(nc.Block())

        def wait(eng, s, value):
            if isinstance(value, int) and value <= 0:
                return
            eng.wait_ge(s, value)

        def wait_apart(eng, s, value):
            eng.wait_ge(s, value)
            eng.sem_inc(waits_apart, 1)

        def sweep(eng, step, spots):
            step(0, 0, False)
            j = 0
            while j < PAIRS:
                if j in spots:
                    spots[j]()
                k = j + 1
                while k < PAIRS - 1 and k not in spots:
                    k += 1
                if k - j > 1:
                    with eng.Fori(j, k) as r:
                        step(2 * r + 1, 1, False)
                        step(2 * r + 2, 0, False)
                else:
                    step(2 * j + 1, 1, False)
                    step(2 * j + 2, 0, j == PAIRS - 1)
                j = k

        def chunks(eng, body):
            body(0, 0, WIDE)
            with eng.Fori(0, 2) as i:
                body(2 * i + 1, 1, WIDE)
                body(2 * i + 2, 0, WIDE)
            body(5, 1, WIDE)
            body(6, 0, NARROW)

        def first(c):
            return isinstance(c, int) and c == 0

        @block.sync
        def _(sp):
            sp.dma_start(x32[:, 0:NB - 1, :], x[0:(NB - 1) * P, :].rearrange("(b p) d -> p b d", p=P)).then_inc(x_loaded, 16)
            sp.wait_ge(const_made, 2)
            sp.dma_start(x32[0:TAIL_A, NB - 1, :], x[(NB - 1) * P:(NB - 1) * P + TAIL_A, :]).then_inc(x_loaded, 16)
            sp.dma_start(x32[TAIL_A:TAIL, NB - 1, :], x[(NB - 1) * P + TAIL_A:N, :]).then_inc(x_loaded, 16)
            sp.dma_start(raw[:, 0, 0:N], adj[0:P, :]).then_inc(raw_loaded[0], 16)
            sp.dma_start(raw[:, 1, 0:N], adj[P:2 * P, :]).then_inc(raw_loaded[1], 16)
            with sp.Fori(1, HALVES - 1) as h:
                for s in range(2):
                    sp.wait_ge(cast_done, 2 * h - 1 + s)
                    sp.dma_start(raw[:, s, 0:N], adj[bass.ds((2 * h + s) * P, P), :]).then_inc(raw_loaded[s], 16)
            sp.wait_ge(cast_done, NB - 3)
            sp.dma_start(raw[:, 0, 0:N], adj[(NB - 2) * P:(NB - 1) * P, :]).then_inc(raw_loaded[0], 16)
            sp.wait_ge(cast_done, NB - 2)
            sp.dma_start(raw[0:TAIL_A, 1, 0:N], adj[(NB - 1) * P:(NB - 1) * P + TAIL_A, :]).then_inc(raw_loaded[1], 16)
            sp.dma_start(raw[TAIL_A:TAIL, 1, 0:N], adj[(NB - 1) * P + TAIL_A:N, :]).then_inc(raw_loaded[1], 16)
            sp.wait_ge(y_done, NB)
            sp.dma_start(w02[:, :, :], w2.rearrange("(k p) o -> p k o", p=P)).then_inc(w2_loaded, 16)
            sp.dma_start(bias02[:, :], b2.partition_broadcast(P)).then_inc(w2_loaded, 16)
            sp.wait_ge(dot_done, 2 * NB)
            sp.dma_start(vrow[:, 0, :], wa[0, D:2 * D].partition_broadcast(P)).then_inc(wx_loaded, 16)
            sp.dma_start(vrow[:, 1, :], wb[0, D:2 * D].partition_broadcast(P)).then_inc(wx_loaded, 16)
            with sp.Fori(0, CH - 1) as c:
                sp.wait_ge(x_done, 3 * NB + 4 * c + 4)
                sp.dma_start(out[bass.ds(c * WIDE, WIDE), :].rearrange("(b p) d -> p b d", p=P),
                             x32[:, bass.ds(4 * c, 4), :]).then_inc(out_stored, 16)
            sp.wait_ge(x_done, 4 * NB)
            sp.dma_start(out[(NB - 2) * P:(NB - 1) * P, :], x32[:, NB - 2, :]).then_inc(out_stored, 16)
            sp.dma_start(out[(NB - 1) * P:(NB - 1) * P + TAIL_A, :], x32[0:TAIL_A, NB - 1, :]).then_inc(out_stored, 16)
            sp.dma_start(out[(NB - 1) * P + TAIL_A:N, :], x32[TAIL_A:TAIL, NB - 1, :]).then_inc(out_stored, 16)
            sp.wait_ge(out_stored, 16 * (CH + 2))

        @block.gpsimd
        def _(pool):
            g = nc.gpsimd
            g.memset(x32[:, NB - 1, :], 0.0).then_inc(const_made, 1)
            g.memset(raw[:, :, N:NP], 0.0).then_inc(const_made, 1)
            g.memset(idf[:, :], 0.0).then_inc(const_made, 1)
            g.memset(pad[:, :], 0.0).then_inc(const_made, 1)
            pool.wait_ge(const_made, 4)
            g.affine_select(out=idf[:, :], in_=idf[:, :], compare_op=ALU.not_equal, fill=1.0, base=0,
                            pattern=[[-1, P]], channel_multiplier=1).then_inc(const_made, 1)
            g.affine_select(out=pad[:, :], in_=pad[:, :], compare_op=ALU.not_equal, fill=1.0, base=-N,
                            pattern=[[P, NB]], channel_multiplier=1).then_inc(const_made, 1)
            g.memset(ones[:, :], 1.0).then_inc(const_made, 1)
            g.memset(onesb[:, :], 1.0).then_inc(const_made, 1)
            g.memset(mhalf[:, :], -0.5).then_inc(const_made, 1)
            g.memset(half[:, :], 0.5).then_inc(const_made, 1)
            g.memset(eps[:, :], EPS).then_inc(const_made, 1)
            g.memset(onecol[:, :], 1.0).then_inc(const_made, 1)
            pool.wait_ge(const_made, 6)
            g.tensor_copy(idb[:, :], idf[:, :]).then_inc(const_made, 1)
            pool.wait_ge(const_made, 13)
            pool.wait_ge(prep_dve, 14)
            g.tensor_tensor(out=kcol[:, 1:2], in0=kcol[:, 0:1], in1=half[:, :], op=ALU.pow).then_inc(prep_pool, 1)
            pool.wait_ge(prep_dve, 15)
            g.partition_all_reduce(mxc[:, 1:2], mxc[:, 0:1], P, bass.bass_isa.ReduceOp.max).then_inc(prep_pool, 1)

            def inverse_deviation(pair):
                pool.wait_ge(mv_done, 2 * pair + 2)
                g.tensor_tensor(out=ve[:, :], in0=mv[:, :, 1], in1=eps[:, :], op=ALU.add).then_inc(ve_done, 1)
                pool.wait_ge(ve_done, pair + 1)
                g.tensor_tensor(out=rstd[:, :], in0=ve[:, :], in1=mhalf[:, 0:2], op=ALU.pow).then_inc(rstd_done, 1)

            def layer0(h, hp):
                def step(q, qp, last):
                    wait(pool, adj_kept, Q * h + q + 1)
                    wait(pool, step_done, Q * h + q - 1)
                    g.tensor_copy(ring[:, (hp + qp) % 2, :, 0:NARROW],
                                  adj_t[:, bass.ds(2 * q, 2), bass.ds(h * NARROW, NARROW)]).then_inc(tile0, 1)
                spots = {1: lambda: None}
                if not first(h):
                    spots = {3: lambda: inverse_deviation(h - 1)}
                sweep(pool, step, spots)

            layer0(0, 0)
            with pool.Fori(0, (HALVES - 1) // 2) as i:
                layer0(2 * i + 1, 1)
                layer0(2 * i + 2, 0)
            pool.wait_ge(cast_done, NB)
            n = [0]

            def column(ins):
                n[0] += 1
                ins.then_inc(cols_pool, 1)
                pool.wait_ge(cols_pool, n[0])
            column(g.tensor_scalar(r3, rowsum, 1.0, None, ALU.add))
            column(g.tensor_scalar(r3b, r3, 1e-30, None, ALU.max))
            column(g.tensor_tensor(out=r3x, in0=r3b, in1=mhalf[:, :], op=ALU.pow))
            column(g.tensor_scalar(r3b, r3, 0.0, None, ALU.is_gt))
            column(g.tensor_tensor(out=r3, in0=r3x, in1=r3b, op=ALU.mult))
            column(g.tensor_scalar(r3x, r3, US, None, ALU.mult))
            column(g.tensor_copy(rpart[:, :, 0], r3x))
            column(g.tensor_tensor(out=rpart[:, :, 1], in0=r3x, in1=rpart[:, :, 0], op=ALU.subtract))
            column(g.tensor_scalar(r3x, r3, XS, None, ALU.mult))
            column(g.tensor_scalar(r3b, r3, 1.0 / XS, None, ALU.mult))
            with pool.Fori(HALVES - 1, 4 * HALVES) as pair:
                inverse_deviation(pair)

        @block.scalar
        def _(act):
            a = nc.scalar
            for k in range(2):
                act.dma_start(w02[:, k, :].rearrange("p (h e) -> p h e", h=HEADS),
                              w0[:, k * P:(k + 1) * P, :].rearrange("h p e -> p h e")).then_inc(w_loaded, 16)
            act.dma_start(wsa[:, :, :], w_sa.rearrange("(k p) o -> p k o", p=P)).then_inc(w_loaded, 16)
            act.dma_start(t_asa, a_sa[0, :].partition_broadcast(P)).then_inc(w_loaded, 16)
            act.dma_start(t_w31, w31).then_inc(w_loaded, 16)
            act.dma_start(t_w32, w32.rearrange("(k p) h -> p k h", p=P)).then_inc(w_loaded, 16)
            act.dma_start(b31c[:, :], b31.rearrange("(p o) -> p o", o=1)).then_inc(w_loaded, 16)
            act.dma_start(bias02[:, :], b0.rearrange("h e -> (h e)").partition_broadcast(P)).then_inc(w_loaded, 16)
            act.dma_start(bias3[:, :], b32.partition_broadcast(P)).then_inc(w_loaded, 16)
            act.dma_start(biasg[:, :], b_gcn.partition_broadcast(P)).then_inc(w_loaded, 16)
            act.dma_start(wg[:, :, :], w_gcn.rearrange("(k p) o -> p k o", p=P)).then_inc(w_loaded, 16)
            act.dma_start(bab[:, 0:1], ba.partition_broadcast(P)).then_inc(w_loaded, 16)
            act.dma_start(bab[:, 1:2], bb.partition_broadcast(P)).then_inc(w_loaded, 16)
            for k in range(2):
                act.dma_start(wgate[:, k, 0:1], wa[0, k * P:(k + 1) * P].rearrange("(p o) -> p o", o=1)).then_inc(w_loaded, 16)
                act.dma_start(wgate[:, k, 1:2], wb[0, k * P:(k + 1) * P].rearrange("(p o) -> p o", o=1)).then_inc(w_loaded, 16)

            def cast(h, hp, last=False):
                for s in range(2):
                    more = 16 if last and s == 1 else 0
                    act.wait_ge(raw_loaded[s], 16 * (h + 1) + more)
                    wait(act, quad_done, Q * (h - 1))
                    a.activation(rawb[:, 2 * hp + s, :], raw[:, s, :], ACT.Copy,
                                 accum_out=rowsum[:, bass.ds(2 * h + s, 1)]).then_inc(cast_done, 1)

            def take_zt(source, sweeps, products, width):
                act.wait_ge(step_done, Q * sweeps)
                wait(act, prod_done, products)
                a.activation(zt[:, :, 0:width], source[:, :, 0:width], ACT.Copy).then_inc(zt_ready, 1)

            cast(0, 0)
            cast(1, 1)
            act.wait_ge(prep_read, 1)
            cast(2, 0)
            take_zt(pairs[0], 1, 0, NARROW)
            with act.Fori(0, (HALVES - 5) // 2) as i:
                for hp in (1, 0):
                    h = 2 * i + 2 - hp
                    cast(h + 2, hp)
                    take_zt(pairs[hp], h + 1, 2 * h, NARROW)
            cast(HALVES - 2, 1)
            take_zt(pairs[1], HALVES - 3, 2 * (HALVES - 4), NARROW)
            cast(HALVES - 1, 0, last=True)
            take_zt(pairs[0], HALVES - 2, 2 * (HALVES - 3), NARROW)
            take_zt(pairs[1], HALVES - 1, 2 * (HALVES - 2), NARROW)

            def adj_tiles(sw, sp_, zi, c, width, spots):
                def step(q, qp, last):
                    act.wait_ge(step_done, Q * sw + q - 1)
                    a.activation(ring[:, (sp_ + qp) % 2, :, 0:width],
                                 adj_t[:, bass.ds(2 * q, 2), bass.ds(c * WIDE, width)], ACT.Copy).then_inc(tile_z, 1)
                sweep(act, step, spots)

            def r_row(c):
                act.wait_ge(m1u_made, Q * (c + 1))
                a.activation(slb[:, :], slb[:, :], ACT.Exp, scale=-0.99, bias=kcol[:, 2:3]).then_inc(rrow_made, 1)

            def tanh_gates(c):
                act.wait_ge(gate_pre, c + 1)
                a.activation(gate[:, :, :], gate[:, :, :], ACT.Tanh, scale=0.5).then_inc(gate_tanh, 1)

            def tanh_block(blk, b):
                act.wait_ge(p1c, blk + 2)
                a.activation(t[:, b % 2, :], t[:, b % 2, :], ACT.Tanh, scale=0.5).then_inc(th_done, 1)

            def column_factors():
                act.wait_ge(cols_dve, 3)
                act.wait_ge(prep_dve, 21)
                a.activation(dcol[:, :], nsr[:, :], ACT.Exp, scale=0.01, bias=kcol[:, 2:3]).then_inc(cols_act, 1)
                a.activation(ccol[:, :], slc[:, :], ACT.Exp, scale=-0.01, bias=kcol[:, 3:4]).then_inc(cols_act, 1)
                a.activation(rcol[:, :], slc[:, :], ACT.Exp, scale=-0.99, bias=kcol[:, 2:3]).then_inc(cols_act, 1)
                a.activation(bcol[:, :], nsr[:, :], ACT.Exp).then_inc(cols_act, 1)

            def layer1(c, cp, width):
                sw = SW1 + 3 * c
                if first(c):
                    spots = {0: lambda: take_zt(pairs[0], SW1, 2 * (HALVES - 1), NARROW), 4: column_factors}
                else:
                    spots = {0: lambda: r_row(c - 1), 1: lambda: tanh_gates(c - 1)}
                    for b in range(4):
                        spots[b + 2] = lambda b=b: tanh_block(4 * (c - 1) + b, b)
                adj_tiles(sw, (1 + cp) % 2, None, c, width, spots)
                take_zt(PZ, sw + 1, NB + 4 * c, width)

                def take_u2():
                    act.wait_ge(step_done, Q * (sw + 2))
                    act.wait_ge(prod_done, NB + 4 * c)
                    act.wait_ge(slb_spread, c + 1)
                    a.activation(ut[:, :, 0:width], PU2[:, :, 0:width], ACT.Copy).then_inc(u2_ready, 1)

                def step(q, qp, last):
                    act.wait_ge(m1u_made, Q * c + q + 1)
                    act.wait_ge(step_done, Q * (sw + 2) + q - 1)
                    slot = (1 + cp + qp) % 2
                    for mi in range(2):
                        ins = a.activation(ring[:, slot, mi, 0:width], m1u[:, slot, mi, 0:width], ACT.Copy,
                                           scale=q2[:, bass.ds(2 * q + mi, 1)])
                    ins.then_inc(tile_u1, 1)
                if first(c):
                    act.wait_ge(cols_dve, 5)
                sweep(act, step, {1: take_u2})

            chunks(act, layer1)

            def layer2(c, cp, width):
                if first(c):
                    spots = {0: lambda: r_row(CH - 1), 1: lambda: tanh_gates(CH - 1),
                             2: lambda: tanh_block(4 * (CH - 1), 0), 3: lambda: tanh_block(4 * (CH - 1) + 1, 1)}
                else:
                    spots = {0: lambda: take_zt(pairs[cp], SW2 + c, 2 * NB + 4 * (c - 1), WIDE)}
                adj_tiles(SW2 + c, (SW2 + cp) % 2, None, c, width, spots)
            chunks(act, layer2)

            def layer3(c, cp, width):
                if first(c):
                    spots = {0: lambda: take_zt(pairs[1], SW3, 2 * NB + 4 * (CH - 1), NARROW)}
                else:
                    spots = {0: lambda: take_zt(pairs[1 - cp], SW3 + c, 3 * NB + 4 * (c - 1), WIDE)}
                adj_tiles(SW3 + c, (SW3 + cp) % 2, None, c, width, spots)
            chunks(act, layer3)
            take_zt(pairs[0], SW3 + CH, 3 * NB + 4 * (CH - 1), NARROW)

        @block.tensor
        def _(pe):
            mm = nc.tensor.matmul
            pe.wait_ge(const_made, 13)
            pe.wait_ge(prep_dve, 8)
            for i in range(4):
                mm(prod[:, i * P:(i + 1) * P], ones[:, :], t_diag[:, i * P:(i + 1) * P], start=True, stop=True)
            pe.wait_ge(w_loaded, 16 * 17)
            for k in range(2):
                ins = nc.tensor.transpose(pairs[0][:, 0, k * P:(k + 1) * P], t_w32[:, k, :], idf[:, :])
            ins.then_inc(prep_pe, 1)
            pe.wait_ge(prep_dve, 10)
            for k in range(2):
                mm(pairs[0][:, 1, k * D:(k + 1) * D], t_w31[:, k * P:(k + 1) * P], t_w32t, start=True, stop=True)
            mm(pairs[1][:, 0, 0:D], t_b31, t_w32t, start=True, stop=True).then_inc(prep_pe, 1)
            pe.wait_ge(prep_read, 1)

            def quads(h, q, qp, hp, last_rows=P):
                bank = (hp + qp) % 2
                wait(pe, adj_kept, Q * h + q - 1)
                for j in range(2):
                    rows = last_rows if j == 1 else P
                    for mi in range(2):
                        blockm = rawb[:, 2 * hp + j, bass.ds((2 * q + mi) * P, P)]
                        nc.tensor.transpose(turned[:, bank, mi * NARROW + j * P:mi * NARROW + (j + 1) * P], blockm, idb[:, :])
                        ins = mm(small[:, bass.ds(2 * q + mi, 1)], rawb[0:rows, 2 * hp + j, bass.ds((2 * q + mi) * P, P)],
                                 onesb[0:rows, :], start=(first(h) and first(q) and j == 0 and mi == 0),
                                 stop=False, skip_group_check=True)
                ins.then_inc(quad_done, 1)

            def sum_step(bank, parts, q, slot, width, is_first, is_last, extra=None):
                for mi in range(2):
                    if extra:
                        extra(q, slot, mi, is_first and mi == 0)
                    for f in range(2):
                        for part in range(2):
                            ins = mm(bank[:, f, 0:width], parts[:, 2 * q + mi, part, f * P:(f + 1) * P],
                                     ring[:, slot, mi, 0:width], start=(is_first and mi == 0 and part == 0),
                                     stop=(is_last and mi == 1 and part == 1), skip_group_check=True)
                ins.then_inc(step_done, 1)

            def products(blk, zt_count, b0, w):
                pe.wait_ge(zt_ready, zt_count)
                wait(pe, y_done, blk)
                for b in range(2):
                    for k in range(2):
                        ins = mm(prodv[:, b, :], zt[:, k, (b0 + b) * P:(b0 + b + 1) * P], w[:, k, :],
                                 start=(k == 0), stop=(k == 1))
                    ins.then_inc(prod_done, 1)

            pe.wait_ge(cast_done, 2)

            def step0(q, qp, last):
                quads(0, q, qp, 0)
            sweep(pe, step0, {1: lambda: None})

            def layer0(h, hp, more=True, last_rows=P):
                if more:
                    pe.wait_ge(cast_done, 2 * h + 4)
                wait(pe, zt_ready, h - 1)
                if first(h):
                    pe.wait_ge(xs_ready, 1)

                def step(q, qp, last):
                    if more:
                        quads(h + 1, q, qp, 1 - hp, last_rows)
                    pe.wait_ge(tile0, Q * h + q + 1)
                    sum_step(pairs[hp], xs, q, (hp + qp) % 2, NARROW, first(q), last)
                spots = {} if first(h) else {1: lambda: products(2 * (h - 1), h, 0, w02)}
                sweep(pe, step, spots)

            layer0(0, 0)
            layer0(1, 1)
            layer0(2, 0)
            with pe.Fori(1, (HALVES - 3) // 2) as i:
                layer0(2 * i + 1, 1)
                layer0(2 * i + 2, 0)
            layer0(HALVES - 2, 1, last_rows=TAIL)
            layer0(HALVES - 1, 0, more=False)

            def attention_products(blk, b):
                pe.wait_ge(p1c, blk + 1)
                for i, (src, w) in enumerate(((zt, wg), (ut, wsa))):
                    for k in range(2):
                        ins = mm(prodv[:, i, :], src[:, k, b * P:(b + 1) * P], w[:, k, :], start=(k == 0), stop=(k == 1))
                ins.then_inc(prod_done, 1)

            def gates_and_first(c, nblocks):
                pe.wait_ge(zt_ready, ZT1 + c + 1)
                for b in range(nblocks):
                    for k in range(2):
                        ins = mm(small[:, 16 + 2 * b:18 + 2 * b], zt[:, k, b * P:(b + 1) * P], wgate[:, k, :],
                                 start=False, stop=False, skip_group_check=True)
                ins.then_inc(gates_done, 1)
                pe.wait_ge(ut_ready, c + 1)
                attention_products(4 * c, 0)

            def layer1(c, cp, width):
                sw = SW1 + 3 * c
                nb = width // P
                p = (1 + cp) % 2

                def spread():
                    pe.wait_ge(diag_made, c + 1)
                    wait(pe, u2_ready, c)
                    for b in range(nb):
                        ins = mm(PU2[:, 0, b * P:(b + 1) * P], ones[:, :], t_diag[:, b * P:(b + 1) * P], start=True, stop=True)
                    ins.then_inc(slb_spread, 1)

                if first(c):
                    pe.wait_ge(zt_ready, ZT1 - 1)
                    pe.wait_ge(adj_kept, Q * HALVES)
                    spots = {1: lambda: products(NB - 2, ZT1, 0, w02), 5: spread}
                else:
                    spots = {1: lambda: gates_and_first(c - 1, 4), 5: spread}
                    for b in range(1, 4):
                        spots[b + 1] = lambda b=b: attention_products(4 * (c - 1) + b, b)

                def zstep(q, qp, last):
                    if first(c):
                        pe.wait_ge(xs_ready, q + 2)
                    pe.wait_ge(tile_z, Q * c + q + 1)
                    sum_step(PZ, xs, q, (p + qp) % 2, width, first(q), last)
                sweep(pe, zstep, spots)

                def weights(cols, parts):
                    def extra(q, slot, mi, start):
                        for b in range(nb):
                            mm(small[:, cols + 2 * b:cols + 2 * b + 2], ring[:, slot, mi, b * P:(b + 1) * P],
                               parts[:, 2 * q + mi, :], start=(start and cols == 0 and b == 0), stop=False,
                               skip_group_check=True)
                    return extra

                pe.wait_ge(slb_ready, c + 1)
                if first(c):
                    pe.wait_ge(deg_read, 1)
                    pe.wait_ge(cols_dve, 15)
                else:
                    pe.wait_ge(small_read, c)

                def u2step(q, qp, last):
                    if first(c):
                        pe.wait_ge(ds_ready, q + 1)
                    pe.wait_ge(tile_u2, Q * c + q + 1)
                    sum_step(PU2, ds, q, (1 + p + qp) % 2, width, first(q), last, weights(0, dpart))
                sweep(pe, u2step, {})

                if first(c):
                    pe.wait_ge(zt_ready, ZT1)
                else:
                    pe.wait_ge(ut_ready, c)

                def u1step(q, qp, last):
                    if first(c):
                        pe.wait_ge(bs_ready, q + 1)
                    pe.wait_ge(tile_u1, Q * c + q + 1)
                    sum_step(PU1, bs, q, (p + qp) % 2, width, first(q), last, weights(8, bpart))
                sweep(pe, u1step, {})

            chunks(pe, layer1)

            def layer2(c, cp, width):
                if first(c):
                    pe.wait_ge(zt_ready, ZT2)
                    spots = {1: lambda: gates_and_first(CH - 1, 2),
                             2: lambda: attention_products(4 * (CH - 1) + 1, 1)}
                else:
                    spots = {2: lambda: products(2 * NB + 4 * (c - 1), ZT2 + c, 0, w02),
                             4: lambda: products(2 * NB + 4 * (c - 1) + 2, ZT2 + c, 2, w02)}
                    pe.wait_ge(ut_ready, CH)
                    pe.wait_ge(zt_ready, ZT2 + c - 1)

                def step(q, qp, last):
                    if first(c):
                        pe.wait_ge(xs_ready, Q + q + 2)
                    pe.wait_ge(tile_z, Q * (CH + c) + q + 1)
                    sum_step(pairs[1 - cp], xs, q, (SW2 + cp + qp) % 2, width, first(q), last)
                if first(c):
                    pass
                sweep(pe, step, spots)
                if first(c):
                    pe.wait_ge(w2_loaded, 32)
            chunks(pe, layer2)

            def layer3(c, cp, width):
                nb = width // P
                qsum = (small[:, 0:8], PU2[:, 0, 0:8])[cp]
                if first(c):
                    pe.wait_ge(small_read, CH)
                    pe.wait_ge(u2_ready, CH)
                    pe.wait_ge(cols_pool, 10)
                    spots = {1: lambda: products(3 * NB - 2, ZT3, 0, w02)}
                else:
                    spots = {2: lambda: products(3 * NB + 4 * (c - 1), ZT3 + c, 0, w3),
                             4: lambda: products(3 * NB + 4 * (c - 1) + 2, ZT3 + c, 2, w3)}
                    pe.wait_ge(q_read, c)
                pe.wait_ge(zt_ready, ZT3 + c - 1)

                def extra(q, slot, mi, start):
                    for b in range(nb):
                        mm(qsum[:, 2 * b:2 * b + 2], ring[:, slot, mi, b * P:(b + 1) * P], rpart[:, 2 * q + mi, :],
                           start=(start and b == 0), stop=False, skip_group_check=True)

                def own():
                    for b in range(nb):
                        mm(qsum[:, 2 * b:2 * b + 2], idb[:, :], rpart[:, 4 * c + b, :], start=False, stop=False,
                           skip_group_check=True)
                        for f in range(2):
                            for part in range(2):
                                mm(pairs[cp][:, f, b * P:(b + 1) * P], xs[:, 4 * c + b, part, f * P:(f + 1) * P],
                                   idb[:, :], start=False, stop=False, skip_group_check=True)
                spots[5] = own

                def step(q, qp, last):
                    if first(c):
                        pe.wait_ge(xs_ready, 2 * Q + q + 2)
                    pe.wait_ge(tile_z, Q * (2 * CH + c) + q + 1)
                    sum_step(pairs[cp], xs, q, (SW3 + cp + qp) % 2, width, first(q), last, extra)
                sweep(pe, step, spots)
            chunks(pe, layer3)
            products(4 * NB - 2, ZT3 + CH, 0, w3)

        @block.vector
        def _(dve):
            v = nc.vector
            made = [0]

            def prep(ins):
                made[0] += 1
                ins.then_inc(prep_dve, 1)
                dve.wait_ge(prep_dve, made[0])

            dve.wait_ge(w_loaded, 16 * 17)
            dve.wait_ge(const_made, 13)
            for side in range(2):
                for k in range(2):
                    prep(v.scalar_tensor_tensor(out=t[:, 0, :], in0=wsa[:, k, :], scalar=1.0,
                                                in1=t_asa[:, side * D:(side + 1) * D], op0=ALU.mult, op1=ALU.mult,
                                                accum_out=vcol[:, 2 * side + k:2 * side + k + 1]))
            for i in range(4):
                prep(v.tensor_scalar(t_diag[:, i * P:(i + 1) * P], idf[:, :], vcol[:, i:i + 1], None, ALU.mult))
            dve.wait_ge(prep_pe, 1)
            prep(v.tensor_copy(t_w32t, pairs[0][:, 0, 0:D]))
            prep(v.tensor_scalar(t_b31, ones[:, :], b31c[:, :], None, ALU.mult))
            prep(v.tensor_copy(vrow[:, :, :], prodv))
            dve.wait_ge(prep_pe, 2)
            prep(v.tensor_copy(w3[:, :, :], pairs[0][:, 1, :].rearrange("p (k d) -> p k d", k=2)))
            prep(v.tensor_tensor(bias3[:, :], pairs[1][:, 0, 0:D], bias3[:, :], ALU.add))
            v.tensor_scalar(bias3[:, :], bias3[:, :], XS / US, None, ALU.mult)
            v.tensor_scalar(biasg[:, :], biasg[:, :], XS, None, ALU.mult).then_inc(prep_read, 1)
            prep(v.scalar_tensor_tensor(out=t[:, 0, :], in0=vrow[:, 1, :], scalar=1.0, in1=vrow[:, 1, :],
                                        op0=ALU.mult, op1=ALU.mult, accum_out=kcol[:, 0:1]))
            dve.wait_ge(x_loaded, 48)
            assert made[0] == 14
            prep(v.tensor_reduce(mxc[:, 0:1], x32[:, :, :].rearrange("p b d -> p (b d)"), AX.X, ALU.max,
                                 apply_absolute_value=True))
            dve.wait_ge(prep_pool, 2)
            prep(v.tensor_scalar(mxc[:, 1:2], mxc[:, 1:2], 2.0 ** -100, None, ALU.max))
            prep(v.tensor_scalar(mxc[:, 2:3].bitcast(I32), mxc[:, 1:2].bitcast(I32), EXPONENT, None, ALU.bitwise_and))
            prep(v.reciprocal(mxc[:, 3:4], mxc[:, 2:3]))
            prep(v.tensor_scalar(mxc[:, 3:4], mxc[:, 3:4], 2.0 ** 14, None, ALU.mult))
            prep(v.tensor_scalar(kcol[:, 2:3], kcol[:, 1:2], -0.16, None, ALU.mult))
            prep(v.tensor_scalar(kcol[:, 3:4], kcol[:, 1:2], 0.16, None, ALU.mult))
            prep(v.tensor_scalar(xs[:, :, 0, :], x32[:, :, :], mxc[:, 3:4], None, ALU.mult))
            v.scalar_tensor_tensor(out=xs[:, :, 1, :], in0=x32[:, :, :], scalar=mxc[:, 3:4], in1=xs[:, :, 0, :],
                                   op0=ALU.mult, op1=ALU.subtract).then_inc(xs_ready, 1)
            prep(v.tensor_scalar(bias02[:, :], bias02[:, :], mxc[:, 3:4], None, ALU.mult))
            prep(v.tensor_scalar(mxc[:, 2:3], mxc[:, 2:3], 2.0 ** -14, None, ALU.mult))
            prep(v.tensor_scalar(sxcol[:, :], onecol[:, :], mxc[:, 2:3], None, ALU.mult))

            def keep(h, q, qp, hp):
                dve.wait_ge(quad_done, Q * h + q + 1)
                v.tensor_copy(adj_t[:, bass.ds(2 * q, 2), bass.ds(h * NARROW, NARROW)],
                              turned[:, (hp + qp) % 2, 0:WIDE].rearrange("p (m n) -> p m n", m=2)).then_inc(adj_kept, 1)

            def normalise(blk, n, pair):
                for b in range(2):
                    wait_apart(dve, y_done, blk + b + 1)
                    v.bn_stats(st[:, b, :], x32[:, n + b, :]).then_inc(st_done, 1)
                for b in range(2):
                    wait_apart(dve, st_done, blk + b + 1)
                    v.bn_aggr(mv[:, b, :], st[:, b, :]).then_inc(mv_done, 1)
                dve.wait_ge(rstd_done, pair + 1)
                for b in range(2):
                    v.tensor_scalar(x32[:, n + b, :], x32[:, n + b, :], mv[:, b, 0:1], rstd[:, b:b + 1],
                                    ALU.subtract, ALU.mult).then_inc(x_done, 1)

            def finish(blk, n, pair, bias, col_a, col_b, affs=None):
                affs = blk if affs is None else affs
                dve.wait_ge(prod_done, blk + 2)
                for b in range(2):
                    v.scalar_tensor_tensor(out=prodv[:, b, :], in0=bias, scalar=col_a[:, bass.ds(n + b, 1)],
                                           in1=prodv[:, b, :], op0=ALU.mult, op1=ALU.add).then_inc(aff_done, 1)
                for b in range(2):
                    dve.wait_ge(aff_done, affs + b + 1)
                    v.scalar_tensor_tensor(out=x32[:, n + b, :], in0=prodv[:, b, :], scalar=col_b[:, bass.ds(n + b, 1)],
                                           in1=x32[:, n + b, :], op0=ALU.mult, op1=ALU.add).then_inc(y_done, 1)
                normalise(blk, n, pair)

            def finish0(h):
                finish(2 * h, 2 * h, h, bias02[:, :], onecol, sxcol)
                for b in range(2):
                    dve.wait_ge(x_done, 2 * h + b + 1)
                    for side, (sign, col) in enumerate(((1.0, slc), (-1.0, nsr))):
                        if b == 1:
                            dve.wait_ge(dot_done, 4 * h + side + 1)
                        v.scalar_tensor_tensor(out=t[:, side, :], in0=x32[:, 2 * h + b, :], scalar=sign,
                                               in1=vrow[:, side, :], op0=ALU.mult, op1=ALU.mult,
                                               accum_out=col[:, bass.ds(2 * h + b, 1)]).then_inc(dot_done, 1)

            def keep0(q, qp, last):
                keep(0, q, qp, 0)
            sweep(dve, keep0, {})

            def layer0(h, hp):
                def step(q, qp, last):
                    keep(h + 1, q, qp, 1 - hp)
                spots = {} if first(h) else {2: lambda: finish0(h - 1)}
                sweep(dve, step, spots)
            layer0(0, 0)
            with dve.Fori(0, (HALVES - 3) // 2) as i:
                layer0(2 * i + 1, 1)
                layer0(2 * i + 2, 0)
            layer0(HALVES - 2, 1)
            dve.wait_ge(quad_done, Q * HALVES)
            v.tensor_copy(degb[:, :], small[:, 0:NB]).then_inc(deg_read, 1)
            finish0(HALVES - 2)

            def parts(done, q, base, scale):
                two = bass.ds(2 * q, 2)
                v.tensor_scalar(xs[:, two, 0, :], x32[:, two, :], scale, None, ALU.mult).then_inc(hi_done, 1)
                dve.wait_ge(hi_done, base + q + 1)
                v.scalar_tensor_tensor(out=xs[:, two, 1, :], in0=x32[:, two, :], scalar=scale, in1=xs[:, two, 0, :],
                                       op0=ALU.mult, op1=ALU.subtract).then_inc(xs_ready, 1)

            def scaled_parts(dest, col, q, his, base, ready):
                for mi in range(2):
                    v.tensor_scalar(dest[:, 2 * q + mi, 0, :], x32[:, 2 * q + mi, :], col[:, bass.ds(2 * q + mi, 1)], None,
                                    ALU.mult).then_inc(his, 1)
                for mi in range(2):
                    dve.wait_ge(his, base + 2 * q + mi + 1)
                    ins = v.scalar_tensor_tensor(out=dest[:, 2 * q + mi, 1, :], in0=x32[:, 2 * q + mi, :],
                                                 scalar=col[:, bass.ds(2 * q + mi, 1)],
                                                 in1=dest[:, 2 * q + mi, 0, :], op0=ALU.mult, op1=ALU.subtract)
                ins.then_inc(ready, 1)

            dve.wait_ge(x_done, NB - 2)
            with dve.Fori(0, Q - 1) as q:
                dve.wait_ge(step_done, Q * (SW1 - 1) + q + 1)
                parts(xs, q, 0, XS)
            finish0(HALVES - 1)
            dve.wait_ge(step_done, Q * SW1)
            parts(xs, Q - 1, 0, XS)
            ncols = [0]

            def cols(ins):
                ncols[0] += 1
                ins.then_inc(cols_dve, 1)
                dve.wait_ge(cols_dve, ncols[0])
            dve.wait_ge(deg_read, 1)
            cols(v.tensor_tensor(degb[:, :], degb[:, :], pad[:, :], ALU.add))
            dve.wait_ge(dot_done, 2 * NB)
            cols(v.reciprocal(degb[:, :], degb[:, :]))
            cols(v.tensor_scalar(degb[:, :], degb[:, :], 1.0 / XS, None, ALU.mult))
            dve.wait_ge(cols_act, 4)
            cols(v.tensor_scalar(bcol[:, :], bcol[:, :], 2.0 ** -120, None, ALU.max))
            cols(v.tensor_scalar(q2[:, :].bitcast(I32), bcol[:, :].bitcast(I32), EXPONENT, None, ALU.bitwise_and))
            cols(v.reciprocal(qcol[:, :], q2[:, :]))
            cols(v.tensor_tensor(bcol[:, :], bcol[:, :], qcol[:, :], ALU.mult))
            cols(v.tensor_scalar(bcol[:, :], bcol[:, :], US, None, ALU.mult))
            cols(v.tensor_scalar(dcol[:, :], dcol[:, :], US, None, ALU.mult))
            cols(v.tensor_scalar(ccol[:, :], ccol[:, :], 1.0 / US, None, ALU.mult))
            cols(v.tensor_copy(dpart[:, :, 0], dcol[:, :]))
            cols(v.tensor_tensor(dpart[:, :, 1], dcol[:, :], dpart[:, :, 0], ALU.subtract))
            cols(v.tensor_copy(bpart[:, :, 0], bcol[:, :]))
            cols(v.tensor_tensor(bpart[:, :, 1], bcol[:, :], bpart[:, :, 0], ALU.subtract))
            cols(v.memset(xab[:, :, :], 0.0))
            v.memset(sm[:, :], 0.0).then_inc(p1c, 1)

            NCOL = 9

            def attention_columns(c, nblocks):
                k = [0]

                def link(ins):
                    k[0] += 1
                    ins.then_inc(chunk_cols, 1)
                    dve.wait_ge(chunk_cols, NCOL * c + k[0])
                for b in range(nblocks):
                    for side in range(2):
                        if b > 0:
                            dve.wait_ge(xab_dots, 8 * c + 2 * b + side - 1)
                        v.scalar_tensor_tensor(out=t[:, side, :], in0=x32[:, 4 * c + b, :], scalar=1.0,
                                               in1=vrow[:, side, :], op0=ALU.mult, op1=ALU.mult,
                                               accum_out=xab[:, b, side:side + 1]).then_inc(xab_dots, 1)
                dve.wait_ge(xab_dots, 8 * c + 2 * nblocks)
                link(v.tensor_tensor(xab[:, :, :], xab[:, :, :], bab[:, :].unsqueeze(1).broadcast_to([P, 4, 2]), ALU.add))
                dve.wait_ge(gates_done, c + 1)
                w = 2 * nblocks
                for o in (0, 8, 16):
                    ins = v.tensor_copy(sm[:, o:o + w], small[:, o:o + w])
                ins.then_inc(small_read, 1)
                dve.wait_ge(small_read, c + 1)
                v.scalar_tensor_tensor(out=gate[:, :, :], in0=sm[:, 16:24].rearrange("p (b s) -> p b s", s=2),
                                       scalar=1.0 / XS, in1=xab[:, :, :], op0=ALU.mult, op1=ALU.add).then_inc(gate_pre, 1)
                sv = sm[:, 0:16].rearrange("p (b s) -> p b s", s=2)
                link(v.tensor_tensor(dsum[:, :], sv[:, :, 0], sv[:, :, 1], ALU.add))
                four = bass.ds(4 * c, nblocks)
                n4 = slice(0, nblocks)
                link(v.tensor_tensor(den[:, n4], dsum[:, 4:4 + nblocks], rcol[:, four], ALU.mult))
                link(v.tensor_tensor(den[:, n4], den[:, n4], dsum[:, n4], ALU.add))
                link(v.tensor_tensor(den[:, n4], den[:, n4], ccol[:, four], ALU.mult))
                link(v.tensor_scalar(den[:, n4], den[:, n4], 1e-5, None, ALU.add))
                link(v.reciprocal(den[:, n4], den[:, n4]))
                link(v.tensor_tensor(coef[:, n4, 0], den[:, n4], ccol[:, four], ALU.mult))
                dve.wait_ge(gate_tanh, c + 1)
                link(v.tensor_scalar(gate[:, :, :], gate[:, :, :], 0.5, 0.5, ALU.mult, ALU.add))
                v.tensor_tensor(coef[:, n4, 0], coef[:, n4, 0], gate[:, n4, 0], ALU.mult)
                v.tensor_scalar(coef[:, n4, 1], gate[:, n4, 1], 1.0 / XS, None, ALU.mult).then_inc(q_col, 1)
                assert k[0] == NCOL
                dve.wait_ge(q_col, c + 1)

            def mix(blk, b):
                dve.wait_ge(prod_done, NB + blk + 1)
                v.tensor_tensor(t[:, b % 2, :], prodv[:, 0, :], biasg[:, :], ALU.add).then_inc(p1a, 1)
                dve.wait_ge(p1a, blk + 1)
                v.tensor_scalar(t[:, b % 2, :], t[:, b % 2, :], coef[:, b, 1:2], None, ALU.mult).then_inc(p1b, 1)
                dve.wait_ge(p1b, blk + 1)
                v.scalar_tensor_tensor(out=t[:, b % 2, :], in0=prodv[:, 1, :], scalar=coef[:, b, 0:1], in1=t[:, b % 2, :],
                                       op0=ALU.mult, op1=ALU.add).then_inc(p1c, 1)

            def finish1(c, b0):
                mix(4 * c + b0, b0)
                mix(4 * c + b0 + 1, b0 + 1)
                for b in range(2):
                    dve.wait_ge(th_done, 4 * c + b0 + b + 1)
                    v.tensor_scalar(t[:, b, :], t[:, b, :], 0.5, 0.5, ALU.mult, ALU.add).then_inc(sg_done, 1)
                for b in range(2):
                    dve.wait_ge(sg_done, 4 * c + b0 + b + 1)
                    v.tensor_tensor(x32[:, 4 * c + b0 + b, :], x32[:, 4 * c + b0 + b, :], t[:, b, :],
                                    ALU.add).then_inc(y_done, 1)
                normalise(NB + 4 * c + b0, 4 * c + b0, HALVES + 2 * c + b0 // 2)

            def layer1(c, cp, width):
                sw = SW1 + 3 * c
                nb = width // P
                p = (1 + cp) % 2
                if not first(c):
                    attention_columns(c - 1, 4)
                    finish1(c - 1, 0)
                    finish1(c - 1, 2)
                dve.wait_ge(prod_done, NB + 4 * c)
                for b in range(nb):
                    ins = v.tensor_scalar(t_diag[:, b * P:(b + 1) * P], idf[:, :], slc[:, bass.ds(4 * c + b, 1)], None, ALU.mult)
                ins.then_inc(diag_made, 1)
                dve.wait_ge(slb_spread, c + 1)
                v.tensor_copy(slb[:, 0:width], PU2[:, 0, 0:width]).then_inc(slb_ready, 1)
                dve.wait_ge(slb_ready, c + 1)

                def mask(dest, mi, q, op):
                    return v.scalar_tensor_tensor(out=dest, in0=slb[:, 0:width], scalar=nsr[:, bass.ds(2 * q + mi, 1)],
                                                  in1=adj_t[:, 2 * q + mi, bass.ds(c * WIDE, width)], op0=op, op1=ALU.mult)

                def u2step(q, qp, last):
                    if first(c):
                        scaled_parts(ds, dcol, q, dhi_done, 0, ds_ready)
                    dve.wait_ge(step_done, Q * (sw + 1) + q - 1)
                    for mi in range(2):
                        ins = mask(ring[:, (1 + p + qp) % 2, mi, 0:width], mi, q, ALU.is_le)
                    ins.then_inc(tile_u2, 1)
                sweep(dve, u2step, {})

                def u1step(q, qp, last):
                    if first(c):
                        scaled_parts(bs, bcol, q, bhi_done, 0, bs_ready)
                    if not (first(c) and isinstance(q, int) and q < 2):
                        dve.wait_ge(tile_u1, Q * c + q - 1)
                    for mi in range(2):
                        ins = mask(m1u[:, (p + qp) % 2, mi, 0:width], mi, q, ALU.is_gt)
                    ins.then_inc(m1u_made, 1)
                sweep(dve, u1step, {1: lambda: None} if first(c) else {})

                dve.wait_ge(rrow_made, c + 1)
                dve.wait_ge(step_done, Q * (sw + 3))
                for f in range(2):
                    v.tensor_tensor(PU1[:, f, 0:width], PU1[:, f, 0:width], slb[:, 0:width], ALU.mult).then_inc(ru_done, 1)
                dve.wait_ge(u2_ready, c + 1)
                for f in range(2):
                    dve.wait_ge(ru_done, 2 * c + f + 1)
                    ins = v.tensor_tensor(ut[:, f, 0:width], ut[:, f, 0:width], PU1[:, f, 0:width], ALU.add)
                ins.then_inc(ut_ready, 1)
            chunks_dve1 = layer1
            dve.wait_ge(wx_loaded, 32)
            chunks(dve, chunks_dve1)

            dve.wait_ge(x_done, 2 * NB - 2)
            dve.wait_ge(step_done, Q * (SW2 - 2))
            with dve.Fori(0, Q - 1) as q:
                parts(xs, q, Q, XS)
            attention_columns(CH - 1, 2)
            finish1(CH - 1, 0)
            dve.wait_ge(x_done, 2 * NB)
            parts(xs, Q - 1, Q, XS)
            dve.wait_ge(w2_loaded, 32)
            v.tensor_scalar(bias02[:, :], bias02[:, :], XS, None, ALU.mult).then_inc(q_read, 1)
            dve.wait_ge(q_read, 1)

            def finish_chunk(L, c, bias, col_a, col_b):
                for b0 in (0, 2):
                    finish(L * NB + 4 * c + b0, 4 * c + b0, L * HALVES + 2 * c + b0 // 2, bias, col_a, col_b,
                           (L - 1) * NB + 4 * c + b0)

            with dve.Fori(0, CH - 1) as c:
                finish_chunk(2, c, bias02[:, :], rowsum, degb)

            dve.wait_ge(x_done, 3 * NB - 2)
            dve.wait_ge(cols_pool, 10)
            with dve.Fori(0, Q - 1) as q:
                dve.wait_ge(step_done, Q * (SW3 - 1) + q + 1)
                scaled_parts(xs, r3x, q, hi_done, 2 * Q, xs_ready)
            finish(3 * NB - 2, NB - 2, 3 * HALVES - 1, bias02[:, :], rowsum, degb, 2 * NB - 2)
            dve.wait_ge(x_done, 3 * NB)
            dve.wait_ge(step_done, Q * SW3)
            scaled_parts(xs, r3x, Q - 1, hi_done, 2 * Q, xs_ready)

            def q_column(c, cp, nblocks):
                dve.wait_ge(step_done, Q * (SW3 + c + 1))
                qsum = (small[:, 0:2 * nblocks], PU2[:, 0, 0:2 * nblocks])[cp]
                v.tensor_copy(qs_sb[:, 0:2 * nblocks], qsum).then_inc(q_read, 1)
                dve.wait_ge(q_read, c + 2)
                qv = qs_sb[:, 0:2 * nblocks].rearrange("p (b s) -> p b s", s=2)
                v.tensor_tensor(qcol[:, bass.ds(4 * c, nblocks)], qv[:, :, 0], qv[:, :, 1], ALU.add).then_inc(q_col, 1)
                dve.wait_ge(q_col, CH + c + 1)

            with dve.Fori(0, 3) as i:
                for cp in range(2):
                    q_column(2 * i + cp, cp, 4)
                    finish_chunk(3, 2 * i + cp, bias3[:, :], qcol, r3b)
            q_column(CH - 1, 0, 2)
            finish(4 * NB - 2, NB - 2, 4 * HALVES - 1, bias3[:, :], qcol, r3b, 3 * NB - 2)


_INS = ['x', 'adj', 'L0_gnn_W', 'L0_gnn_b', 'L1_gnn_W_sa', 'L1_gnn_a_sa', 'L1_gnn_W_gcnb', 'L1_gnn_b_gcnb',
        'L1_gnn_Wa', 'L1_gnn_ba', 'L1_gnn_Wb', 'L1_gnn_bb', 'L2_gnn_W', 'L2_gnn_b',
        'L3_gnn_W1', 'L3_gnn_b1', 'L3_gnn_W2', 'L3_gnn_b2']


def kernel(**inputs):
    import numpy as _np
    import concourse.bacc as _bacc
    from concourse import mybir as _mybir
    from concourse.bass_utils import run_bass_kernel_spmd as _run

    nc = _bacc.Bacc("TRN2", target_bir_lowering=False, num_devices=1, dynamic_dma_scratch_size=256)
    arrays, args = {}, []
    for name in _INS:
        a = _np.ascontiguousarray(inputs[name])
        arrays[f"in_{name}_dram"] = a
        args.append(nc.dram_tensor(f"in_{name}_dram", a.shape, _mybir.dt.from_np(a.dtype), kind="ExternalInput").ap())
    shape = tuple(inputs['x'].shape)
    args.append(nc.dram_tensor("out_0_dram", shape, _mybir.dt.float32, kind="ExternalOutput").ap())
    four_graph_layers(nc, *args)
    r = _run(nc, [arrays], core_ids=[0])
    return r.results[0]["out_0_dram"]
```

```python
import concourse.bass as bass
from concourse import mybir
from contextlib import ExitStack
import math


def four_graph_layers(nc, x, adj, w0, b0, w_sa, a_sa, w_gcn, b_gcn, wa, ba, wb, bb, w2, b2,
                      w31, b31, w32, b32, out):
    F32, BF16, F16 = mybir.dt.float32, mybir.dt.bfloat16, mybir.dt.float16
    U8, I32 = mybir.dt.uint8, mybir.dt.int32
    ALU, ACT, AX = mybir.AluOpType, mybir.ActivationFunctionType, mybir.AxisListType

    P = 128
    N, D = x.shape
    NB = (N + P - 1) // P
    NP = NB * P
    TAIL = N - (NB - 1) * P
    TAIL_A = TAIL // 16 * 16
    Q = NB // 2
    PAIRS = (Q - 1) // 2
    WIDE, NARROW = 512, 256
    CH = NP // WIDE + 1
    HALVES = NP // NARROW
    HEADS, DPH = w0.shape[0], w0.shape[2]
    EPS = 1e-5
    XS = 2.0 ** 11
    US = 2.0 ** 10
    LN_WS = 15 * math.log(2.0)
    EARLY = 7
    EXPONENT = 0x7F800000
    assert D == 2 * P and NB % 2 == 0 and PAIRS == 6 and (CH - 1) * WIDE + NARROW == NP

    SW1 = HALVES
    SW2 = SW1 + CH
    SW3 = SW2 + CH
    ZT1 = HALVES
    ZT2 = ZT1 + CH
    ZT3 = ZT2 + CH

    ctx = ExitStack()
    with ctx:
        def sb(name, shape, dt):
            return ctx.enter_context(nc.sbuf_tensor(name, shape, dt))

        def sem(name):
            return ctx.enter_context(nc.semaphore(name))

        adj_t = sb("adj_t", [P, NB, NP], U8)
        x32 = sb("x32", [P, NB, D], F32)
        xs = sb("xs", [P, NB, 2, D], F16)
        zone = sb("zone", [P, 2 * NP * 2 * 2], BF16)
        raw = zone[:, 0:4 * NP].bitcast(F32).rearrange("p (s n) -> p s n", s=2)
        rawb = zone[:, 4 * NP:8 * NP].rearrange("p (s n) -> p s n", s=4)
        wf = zone[:, 0:8 * WIDE].bitcast(F32).rearrange("p (s m n) -> p s m n", s=2, m=2)
        wsum = zone[:, 8 * WIDE:16 * WIDE].bitcast(F32).rearrange("p (s m n) -> p s m n", s=2, m=2)
        wr = zone[:, 16 * WIDE:24 * WIDE].bitcast(F16).rearrange("p (s t m n) -> p s t m n", s=2, t=2, m=2)
        xs2 = zone[:, 24 * WIDE:24 * WIDE + EARLY * 4 * D].bitcast(F16).rearrange("p (m t d) -> p m t d", t=2, d=D)
        w02 = sb("w02", [P, 2, D], F32)
        wg = sb("wg", [P, 2, D], F32)
        wgate = sb("wgate", [P, 2, 2], F32)
        wsa = sb("wsa", [P, 2, D], F32)
        w3 = sb("w3", [P, 2, D], F32)
        bias02 = sb("bias02", [P, D], F32)
        biasg = sb("biasg", [P, D], F32)
        bias3 = sb("bias3", [P, D], F32)
        vrow = sb("vrow", [P, 2, D], F32)
        idf = sb("idf", [P, P], F32)
        idb = sb("idb", [P, P], BF16)
        ones = sb("ones", [P, P], F32)
        mhalf = sb("mhalf", [P, NB], F32)
        pad = sb("pad", [P, NB], F32)
        zt = sb("zt", [P, 2, WIDE], F32)
        ut = sb("ut", [P, 2, WIDE], F32)
        slb = sb("slb", [P, 2, WIDE], F32)
        ring = sb("ring", [P, 2, 2, WIDE], BF16)
        t = sb("t", [P, 2, D], F32)
        columns = sb("columns", [P, 11, NB], F32)
        (rowsum, slc, nsr, wcap, wbias, ccol, degb, r3, r3x, r3b, qcol) = (columns[:, i, :] for i in range(11))
        sxcol, onecol = degb, qcol
        degp = sb("degp", [P, CH * NB], F32)
        rpart = sb("rpart", [P, NB, 2], F16)
        little = sb("little", [P, 120], F32)
        taken = [0]

        def piece(*shape):
            size = 1
            for s in shape:
                size *= s
            taken[0] += size
            ap = little[:, taken[0] - size:taken[0]]
            return ap if len(shape) == 1 else ap.rearrange("p (a b) -> p a b", a=shape[0])
        vcol, kcol, mxc, bab, b31c = piece(4), piece(4), piece(4), piece(2), piece(1)
        st, mv, ve, rstd = piece(2, 6), piece(2, 2), piece(2), piece(2)
        sm, den, qs_sb, slq = piece(12), piece(4), piece(8), piece(4)
        xab, gate, coef = piece(4, 2), piece(4, 2), piece(4, 2)
        half, eps = piece(1), piece(2)

        pairs = [ctx.enter_context(nc.psum_tensor(f"sum{i}", [P, 2, WIDE], F32)) for i in range(3)]
        prod = ctx.enter_context(nc.psum_tensor("prod", [P, WIDE], F32))
        small = ctx.enter_context(nc.psum_tensor("small", [P, WIDE], F32))
        turned = pairs[2][:, :, :].bitcast(BF16)
        PZ = pairs[1]
        PA = (pairs[2], pairs[0])
        prodv = prod[:, :].rearrange("p (b d) -> p b d", b=2)

        t_asa = zt[:, 0, :]
        t_diag = ut[:, 0, :]
        t_w31 = ut[:, 1, 0:D]
        t_w32 = ut[:, 1, D:2 * D].rearrange("p (k h) -> p k h", k=2)
        t_w32t = slb[:, 0, 0:D]
        t_b31 = slb[:, 0, D:D + P]

        x_loaded, w_loaded, w2_loaded, wx_loaded = sem("x_loaded"), sem("w_loaded"), sem("w2_loaded"), sem("wx_loaded")
        raw_loaded = [sem("raw_loaded0"), sem("raw_loaded1")]
        out_stored = sem("out_stored")
        const_made = sem("const_made")
        prep_dve, prep_pe, prep_read, prep_pool = sem("prep_dve"), sem("prep_pe"), sem("prep_read"), sem("prep_pool")
        cast_done, quad_done, adj_kept = sem("cast_done"), sem("quad_done"), sem("adj_kept")
        tile0, tile_z = sem("tile0"), sem("tile_z")
        exp_done, masked, w_high, w_low, w_added = (sem("exp_done"), sem("masked"), sem("w_high"), sem("w_low"),
                                                    sem("w_added"))
        step_done, z_done = sem("step_done"), sem("z_done")
        zt_ready, ut_ready = sem("zt_ready"), sem("ut_ready")
        prod_done, aff_done, y_done, st_done, mv_done = (sem("prod_done"), sem("aff_done"), sem("y_done"),
                                                         sem("st_done"), sem("mv_done"))
        ve_done, rstd_done, x_done = sem("ve_done"), sem("rstd_done"), sem("x_done")
        dot_done = sem("dot_done")
        hi_done, xs_ready = sem("hi_done"), sem("xs_ready")
        cols_dve, cols_act, cols_pool = sem("cols_dve"), sem("cols_act"), sem("cols_pool")
        slq_made, slb_spread, slb_ready = sem("slq_made"), sem("slb_spread"), sem("slb_ready")
        gates_done, small_read, gate_pre, gate_tanh, chunk_cols = (sem("gates_done"), sem("small_read"), sem("gate_pre"),
                                                                   sem("gate_tanh"), sem("chunk_cols"))
        p1a, p1b, p1c, th_done = sem("p1a"), sem("p1b"), sem("p1c"), sem("th_done")
        q_read, q_col = sem("q_read"), sem("q_col")

        waits_apart, xab_dots = sem("waits_apart"), sem("xab_dots")

        block = ctx.enter_context(nc.Block())

        def wait(eng, s, value):
            if isinstance(value, int) and value <= 0:
                return
            eng.wait_ge(s, value)

        def wait_apart(eng, s, value):
            eng.wait_ge(s, value)
            eng.sem_inc(waits_apart, 1)

        def sweep(eng, step, spots):
            step(0, 0, False)
            j = 0
            while j < PAIRS:
                if j in spots:
                    spots[j]()
                k = j + 1
                while k < PAIRS - 1 and k not in spots:
                    k += 1
                if k - j > 1:
                    with eng.Fori(j, k) as r:
                        step(2 * r + 1, 1, False)
                        step(2 * r + 2, 0, False)
                else:
                    step(2 * j + 1, 1, False)
                    step(2 * j + 2, 0, j == PAIRS - 1)
                j = k

        def chunks(eng, body):
            body(0, 0, WIDE)
            with eng.Fori(0, 2) as i:
                body(2 * i + 1, 1, WIDE)
                body(2 * i + 2, 0, WIDE)
            body(5, 1, WIDE)
            body(6, 0, NARROW)

        def first(c):
            return isinstance(c, int) and c == 0

        @block.sync
        def _(sp):
            sp.dma_start(x32[:, 0:NB - 1, :], x[0:(NB - 1) * P, :].rearrange("(b p) d -> p b d", p=P)).then_inc(x_loaded, 16)
            sp.wait_ge(const_made, 2)
            sp.dma_start(x32[0:TAIL_A, NB - 1, :], x[(NB - 1) * P:(NB - 1) * P + TAIL_A, :]).then_inc(x_loaded, 16)
            sp.dma_start(x32[TAIL_A:TAIL, NB - 1, :], x[(NB - 1) * P + TAIL_A:N, :]).then_inc(x_loaded, 16)
            sp.dma_start(raw[:, 0, 0:N], adj[0:P, :]).then_inc(raw_loaded[0], 16)
            sp.dma_start(raw[:, 1, 0:N], adj[P:2 * P, :]).then_inc(raw_loaded[1], 16)
            with sp.Fori(1, HALVES - 1) as h:
                for s in range(2):
                    sp.wait_ge(cast_done, 2 * h - 1 + s)
                    sp.dma_start(raw[:, s, 0:N], adj[bass.ds((2 * h + s) * P, P), :]).then_inc(raw_loaded[s], 16)
            sp.wait_ge(cast_done, NB - 3)
            sp.dma_start(raw[:, 0, 0:N], adj[(NB - 2) * P:(NB - 1) * P, :]).then_inc(raw_loaded[0], 16)
            sp.wait_ge(cast_done, NB - 2)
            sp.dma_start(raw[0:TAIL_A, 1, 0:N], adj[(NB - 1) * P:(NB - 1) * P + TAIL_A, :]).then_inc(raw_loaded[1], 16)
            sp.dma_start(raw[TAIL_A:TAIL, 1, 0:N], adj[(NB - 1) * P + TAIL_A:N, :]).then_inc(raw_loaded[1], 16)
            sp.wait_ge(y_done, NB)
            sp.dma_start(w02[:, :, :], w2.rearrange("(k p) o -> p k o", p=P)).then_inc(w2_loaded, 16)
            sp.dma_start(bias02[:, :], b2.partition_broadcast(P)).then_inc(w2_loaded, 16)
            sp.wait_ge(dot_done, 2 * NB)
            sp.dma_start(vrow[:, 0, :], wa[0, D:2 * D].partition_broadcast(P)).then_inc(wx_loaded, 16)
            sp.dma_start(vrow[:, 1, :], wb[0, D:2 * D].partition_broadcast(P)).then_inc(wx_loaded, 16)
            with sp.Fori(0, CH - 1) as c:
                sp.wait_ge(x_done, 3 * NB + 4 * c + 4)
                sp.dma_start(out[bass.ds(c * WIDE, WIDE), :].rearrange("(b p) d -> p b d", p=P),
                             x32[:, bass.ds(4 * c, 4), :]).then_inc(out_stored, 16)
            sp.wait_ge(x_done, 4 * NB)
            sp.dma_start(out[(NB - 2) * P:(NB - 1) * P, :], x32[:, NB - 2, :]).then_inc(out_stored, 16)
            sp.dma_start(out[(NB - 1) * P:(NB - 1) * P + TAIL_A, :], x32[0:TAIL_A, NB - 1, :]).then_inc(out_stored, 16)
            sp.dma_start(out[(NB - 1) * P + TAIL_A:N, :], x32[TAIL_A:TAIL, NB - 1, :]).then_inc(out_stored, 16)
            sp.wait_ge(out_stored, 16 * (CH + 2))

        @block.gpsimd
        def _(pool):
            g = nc.gpsimd
            g.memset(x32[:, NB - 1, :], 0.0).then_inc(const_made, 1)
            g.memset(raw[:, :, N:NP], 0.0).then_inc(const_made, 1)
            g.memset(idf[:, :], 0.0).then_inc(const_made, 1)
            g.memset(pad[:, :], 0.0).then_inc(const_made, 1)
            pool.wait_ge(const_made, 4)
            g.affine_select(out=idf[:, :], in_=idf[:, :], compare_op=ALU.not_equal, fill=1.0, base=0,
                            pattern=[[-1, P]], channel_multiplier=1).then_inc(const_made, 1)
            g.affine_select(out=pad[:, :], in_=pad[:, :], compare_op=ALU.not_equal, fill=1.0, base=-N,
                            pattern=[[P, NB]], channel_multiplier=1).then_inc(const_made, 1)
            g.memset(ones[:, :], 1.0).then_inc(const_made, 1)
            g.memset(mhalf[:, :], -0.5).then_inc(const_made, 1)
            g.memset(half[:, :], 0.5).then_inc(const_made, 1)
            g.memset(eps[:, :], EPS).then_inc(const_made, 1)
            g.memset(onecol[:, :], 1.0).then_inc(const_made, 1)
            pool.wait_ge(const_made, 6)
            g.tensor_copy(idb[:, :], idf[:, :]).then_inc(const_made, 1)
            pool.wait_ge(const_made, 12)
            pool.wait_ge(prep_dve, 14)
            g.tensor_tensor(out=kcol[:, 1:2], in0=kcol[:, 0:1], in1=half[:, :], op=ALU.pow).then_inc(prep_pool, 1)
            pool.wait_ge(prep_dve, 15)
            g.partition_all_reduce(mxc[:, 1:2], mxc[:, 0:1], P, bass.bass_isa.ReduceOp.max).then_inc(prep_pool, 1)

            def inverse_deviation(pair):
                pool.wait_ge(mv_done, 2 * pair + 2)
                g.tensor_tensor(out=ve[:, :], in0=mv[:, :, 1], in1=eps[:, :], op=ALU.add).then_inc(ve_done, 1)
                pool.wait_ge(ve_done, pair + 1)
                g.tensor_tensor(out=rstd[:, :], in0=ve[:, :], in1=mhalf[:, 0:2], op=ALU.pow).then_inc(rstd_done, 1)

            with pool.Fori(0, HALVES - 1) as pair:
                inverse_deviation(pair)
            pool.wait_ge(cast_done, NB)
            n = [0]

            def column(ins):
                n[0] += 1
                ins.then_inc(cols_pool, 1)
                pool.wait_ge(cols_pool, n[0])
            column(g.tensor_scalar(r3, rowsum, 1.0, None, ALU.add))
            column(g.tensor_scalar(r3b, r3, 1e-30, None, ALU.max))
            column(g.tensor_tensor(out=r3x, in0=r3b, in1=mhalf[:, :], op=ALU.pow))
            column(g.tensor_scalar(r3b, r3, 0.0, None, ALU.is_gt))
            column(g.tensor_tensor(out=r3, in0=r3x, in1=r3b, op=ALU.mult))
            column(g.tensor_scalar(r3x, r3, US, None, ALU.mult))
            column(g.tensor_copy(rpart[:, :, 0], r3x))
            column(g.tensor_tensor(out=rpart[:, :, 1], in0=r3x, in1=rpart[:, :, 0], op=ALU.subtract))
            column(g.tensor_scalar(r3x, r3, XS, None, ALU.mult))
            column(g.tensor_scalar(r3b, r3, 1.0 / XS, None, ALU.mult))

            pool.wait_ge(tile0, Q * HALVES)
            g.memset(adj_t[:, :, N:NP], 0.0).then_inc(cols_pool, 1)
            pool.wait_ge(cols_pool, 11)
            def layer1(c, cp, width):
                def step(q, qp, last):
                    slot = (1 + cp + qp) % 2
                    wait_apart(pool, masked, Q * c + q + 1)
                    if first(q):
                        if not first(c):
                            wait_apart(pool, step_done, Q * (SW1 + c - 1) + 2)
                        g.tensor_copy(wsum[:, cp, :, 0:width], wf[:, slot, :, 0:width]).then_inc(w_added, 1)
                    else:
                        pool.wait_ge(w_added, Q * c + q)
                        g.tensor_tensor(out=wsum[:, cp, :, 0:width], in0=wsum[:, cp, :, 0:width],
                                        in1=wf[:, slot, :, 0:width], op=ALU.add).then_inc(w_added, 1)
                if first(c):
                    spots = {2: lambda: inverse_deviation(HALVES - 1)}
                else:
                    spots = {4: lambda: inverse_deviation(HALVES + 2 * (c - 1))}
                sweep(pool, step, spots)
                if not first(c):
                    inverse_deviation(HALVES + 2 * (c - 1) + 1)
            chunks(pool, layer1)
            with pool.Fori(2 * HALVES - 1, 4 * HALVES) as pair:
                inverse_deviation(pair)

        @block.scalar
        def _(act):
            a = nc.scalar
            for k in range(2):
                act.dma_start(w02[:, k, :].rearrange("p (h e) -> p h e", h=HEADS),
                              w0[:, k * P:(k + 1) * P, :].rearrange("h p e -> p h e")).then_inc(w_loaded, 16)
            act.dma_start(wsa[:, :, :], w_sa.rearrange("(k p) o -> p k o", p=P)).then_inc(w_loaded, 16)
            act.dma_start(t_asa, a_sa[0, :].partition_broadcast(P)).then_inc(w_loaded, 16)
            act.dma_start(t_w31, w31).then_inc(w_loaded, 16)
            act.dma_start(t_w32, w32.rearrange("(k p) h -> p k h", p=P)).then_inc(w_loaded, 16)
            act.dma_start(b31c[:, :], b31.rearrange("(p o) -> p o", o=1)).then_inc(w_loaded, 16)
            act.dma_start(bias02[:, :], b0.rearrange("h e -> (h e)").partition_broadcast(P)).then_inc(w_loaded, 16)
            act.dma_start(bias3[:, :], b32.partition_broadcast(P)).then_inc(w_loaded, 16)
            act.dma_start(biasg[:, :], b_gcn.partition_broadcast(P)).then_inc(w_loaded, 16)
            act.dma_start(wg[:, :, :], w_gcn.rearrange("(k p) o -> p k o", p=P)).then_inc(w_loaded, 16)
            act.dma_start(bab[:, 0:1], ba.partition_broadcast(P)).then_inc(w_loaded, 16)
            act.dma_start(bab[:, 1:2], bb.partition_broadcast(P)).then_inc(w_loaded, 16)
            for k in range(2):
                act.dma_start(wgate[:, k, 0:1], wa[0, k * P:(k + 1) * P].rearrange("(p o) -> p o", o=1)).then_inc(w_loaded, 16)
                act.dma_start(wgate[:, k, 1:2], wb[0, k * P:(k + 1) * P].rearrange("(p o) -> p o", o=1)).then_inc(w_loaded, 16)

            def cast(h, hp, s, more=0):
                act.wait_ge(raw_loaded[s], 16 * (h + 1) + more)
                wait(act, quad_done, Q * (h - 1))
                a.activation(rawb[:, 2 * hp + s, :], raw[:, s, :], ACT.Copy,
                             accum_out=rowsum[:, bass.ds(2 * h + s, 1)]).then_inc(cast_done, 1)

            def take_zt(source, sweeps, products, width):
                act.wait_ge(step_done, Q * sweeps)
                wait(act, prod_done, products)
                a.activation(zt[:, :, 0:width], source[:, :, 0:width], ACT.Copy).then_inc(zt_ready, 1)

            def x_high(dest, q, scale):
                a.activation(dest[:, bass.ds(2 * q, 2), 0, :], x32[:, bass.ds(2 * q, 2), :], ACT.Copy,
                             scale=scale).then_inc(hi_done, 1)

            def spread_row(c, cp, width):
                act.wait_ge(slb_spread, c + 1)
                a.activation(slb[:, cp, 0:width], PA[cp][:, 0, 0:width], ACT.Copy).then_inc(slb_ready, 1)

            def cap(blocks):
                a.activation(wcap[:, blocks], nsr[:, blocks], ACT.Exp, scale=0.01, bias=kcol[:, 2:3]).then_inc(cols_act, 1)

            def layer0(h, hp, casts=True, more=0, final=False):
                def step(q, qp, last):
                    wait(act, adj_kept, Q * h + q + 1)
                    wait(act, step_done, Q * h + q - 1)
                    a.activation(ring[:, (hp + qp) % 2, :, 0:NARROW],
                                 adj_t[:, bass.ds(2 * q, 2), bass.ds(h * NARROW, NARROW)], ACT.Copy).then_inc(tile0, 1)
                    if final and not (isinstance(q, int) and q < 2):
                        act.wait_ge(step_done, Q * h + q - 1)
                        x_high(xs, q - 2, XS)
                spots = {1: lambda: None}
                if not first(h):
                    spots = {0: lambda: take_zt(pairs[1 - hp], h, 2 * (h - 1), NARROW)}
                if final:
                    spots.update({1: lambda: None, 4: lambda: spread_row(0, 0, WIDE)})
                if casts:
                    spots[2] = lambda: cast(h + 2, hp, 0)
                    spots[4] = lambda: cast(h + 2, hp, 1, more)
                sweep(act, step, spots)

            for h in range(2):
                for s in range(2):
                    cast(h, h, s)
            layer0(0, 0)
            act.wait_ge(prep_read, 1)
            layer0(1, 1)
            layer0(2, 0)
            with act.Fori(1, (HALVES - 5) // 2) as i:
                layer0(2 * i + 1, 1)
                layer0(2 * i + 2, 0)
            layer0(HALVES - 4, 1)
            layer0(HALVES - 3, 0, more=16)
            layer0(HALVES - 2, 1, casts=False)
            act.wait_ge(prep_dve, 21)
            act.wait_ge(x_done, NB - 4)
            layer0(HALVES - 1, 0, casts=False, final=True)

            def adj_tiles(sw, sp_, zi, c, width, spots):
                def step(q, qp, last):
                    act.wait_ge(step_done, Q * sw + q - 1)
                    a.activation(ring[:, (sp_ + qp) % 2, :, 0:width],
                                 adj_t[:, bass.ds(2 * q, 2), bass.ds(c * WIDE, width)], ACT.Copy).then_inc(tile_z, 1)
                sweep(act, step, spots)

            def tanh_gates(c):
                act.wait_ge(gate_pre, c + 1)
                a.activation(gate[:, :, :], gate[:, :, :], ACT.Tanh, scale=0.5).then_inc(gate_tanh, 1)

            def tanh_block(blk, b):
                act.wait_ge(p1c, blk + 2)
                a.activation(t[:, b % 2, :], t[:, b % 2, :], ACT.Tanh, scale=0.5).then_inc(th_done, 1)

            def take_z(c, width):
                act.wait_ge(z_done, Q * (c + 1))
                act.wait_ge(prod_done, NB + 4 * c)
                a.activation(zt[:, :, 0:width], PZ[:, :, 0:width], ACT.Copy).then_inc(zt_ready, 1)

            def take_ut(c, cp, width):
                act.wait_ge(step_done, Q * (SW1 + c + 1))
                act.wait_ge(prod_done, NB + 4 * c)
                a.activation(ut[:, :, 0:width], PA[cp][:, :, 0:width], ACT.Copy).then_inc(ut_ready, 1)

            def last_blocks():
                act.wait_ge(x_done, NB)
                act.wait_ge(step_done, Q * SW1)
                x_high(xs, Q - 1, XS)
                act.wait_ge(dot_done, 2 * NB)
                cap(slice(NB - 2, NB))
                a.activation(ccol[:, :], slc[:, :], ACT.Exp, scale=-0.01, bias=kcol[:, 3:4]).then_inc(cols_act, 1)

            def layer1(c, cp, width):
                slotted = (1 + cp) % 2

                def high(q, slot):
                    act.wait_ge(masked, Q * c + q + 1)
                    if not (first(c) and isinstance(q, int) and q < 2):
                        act.wait_ge(step_done, Q * (SW1 + c) + q - 1)
                    a.activation(wr[:, slot, 0, :, 0:width], wf[:, slot, :, 0:width], ACT.Copy).then_inc(w_high, 1)

                def step(q, qp, last):
                    slot = (slotted + qp) % 2
                    early = first(c) and isinstance(q, int) and q < 2
                    if not early:
                        act.wait_ge(w_low, Q * c + q - 1)
                        act.wait_ge(w_added, Q * c + q - 1)
                    if first(c) and last:
                        act.wait_ge(cols_dve, 2)
                    for mi in range(2):
                        ins = a.activation(wf[:, slot, mi, 0:width], slb[:, cp, 0:width], ACT.Exp, scale=-0.99,
                                           bias=wbias[:, bass.ds(2 * q + mi, 1)])
                    ins.then_inc(exp_done, 1)
                    if not first(q):
                        high(q - 1, 1 - slot)
                    if early:
                        act.wait_ge(step_done, Q * SW1 + q - 1)
                    else:
                        act.wait_ge(z_done, Q * c + q - 1)
                    for mi in range(2):
                        ins = a.activation(ring[:, slot, mi, 0:width], adj_t[:, 2 * q + mi, bass.ds(c * WIDE, width)],
                                           ACT.Copy, accum_out=degp[:, bass.ds(c * NB + 2 * q + mi, 1)])
                    ins.then_inc(tile_z, 1)
                    if isinstance(c, int) and c == CH - 2 and first(q):
                        act.wait_ge(x_done, NB + 2 * EARLY + 2)
                        x_high(xs2, 0, XS)

                def early_pair(j):
                    x_high(xs2, 2 * j + 1, XS)
                    x_high(xs2, 2 * j + 2, XS)

                if first(c):
                    spots = {0: lambda: take_zt(pairs[0], SW1, 2 * (HALVES - 1), NARROW), 1: lambda: None, 4: last_blocks}
                else:
                    spots = {0: lambda: take_z(c - 1, WIDE), 1: lambda: (take_ut(c - 1, 1 - cp, WIDE), tanh_gates(c - 1))}
                    for b in range(4):
                        spots[b + 2] = lambda b=b: tanh_block(4 * (c - 1) + b, b)
                    if isinstance(c, int) and c == CH - 2:
                        take = spots[0]
                        spots[0] = lambda: (take(), early_pair(0))
                        for j in (1, 2):
                            spots[j + 2] = lambda j=j, old=spots[j + 2]: (old(), early_pair(j))
                if not (isinstance(c, int) and c == CH - 1):
                    nextw = NARROW if isinstance(c, int) and c == CH - 2 else WIDE
                    spots[5] = lambda old=spots.get(5, lambda: None): (old(), spread_row(c + 1, 1 - cp, nextw))
                act.wait_ge(slb_ready, c + 1)
                if first(c):
                    act.wait_ge(cols_dve, 1)
                sweep(act, step, spots)
                high(Q - 1, slotted)

            act.wait_ge(dot_done, 2 * (NB - 2))
            cap(slice(0, NB - 2))
            act.wait_ge(x_done, NB - 2)
            act.wait_ge(step_done, Q * (SW1 - 1) + Q - 1)
            x_high(xs, Q - 2, XS)
            chunks(act, layer1)
            take_z(CH - 1, NARROW)
            take_ut(CH - 1, 0, NARROW)

            def later(first_q, end_q, blocks_done):
                act.wait_ge(x_done, blocks_done)
                for q in range(first_q, end_q):
                    x_high(xs, q, XS)

            def layer2(c, cp, width):
                if first(c):
                    spots = {0: lambda: later(EARLY, Q - 3, 2 * NB - 6), 1: lambda: later(Q - 3, Q - 1, 2 * NB - 2),
                             2: lambda: tanh_gates(CH - 1),
                             3: lambda: (tanh_block(4 * (CH - 1), 0), tanh_block(4 * (CH - 1) + 1, 1)),
                             5: lambda: later(Q - 1, Q, 2 * NB)}
                else:
                    spots = {0: lambda: take_zt(pairs[cp], SW2 + c, 2 * NB + 4 * (c - 1), WIDE)}
                adj_tiles(SW2 + c, (SW2 + cp) % 2, None, c, width, spots)
            chunks(act, layer2)

            def layer3(c, cp, width):
                if first(c):
                    spots = {0: lambda: take_zt(pairs[1], SW3, 2 * NB + 4 * (CH - 1), NARROW)}
                else:
                    spots = {0: lambda: take_zt(pairs[1 - cp], SW3 + c, 3 * NB + 4 * (c - 1), WIDE)}
                adj_tiles(SW3 + c, (SW3 + cp) % 2, None, c, width, spots)
            chunks(act, layer3)
            take_zt(pairs[0], SW3 + CH, 3 * NB + 4 * (CH - 1), NARROW)

        @block.tensor
        def _(pe):
            mm = nc.tensor.matmul
            pe.wait_ge(const_made, 12)
            pe.wait_ge(prep_dve, 8)
            for i in range(4):
                mm(prod[:, i * P:(i + 1) * P], ones[:, :], t_diag[:, i * P:(i + 1) * P], start=True, stop=True)
            pe.wait_ge(w_loaded, 16 * 17)
            for k in range(2):
                ins = nc.tensor.transpose(pairs[0][:, 0, k * P:(k + 1) * P], t_w32[:, k, :], idf[:, :])
            ins.then_inc(prep_pe, 1)
            pe.wait_ge(prep_dve, 10)
            for k in range(2):
                mm(pairs[0][:, 1, k * D:(k + 1) * D], t_w31[:, k * P:(k + 1) * P], t_w32t, start=True, stop=True)
            mm(pairs[1][:, 0, 0:D], t_b31, t_w32t, start=True, stop=True).then_inc(prep_pe, 1)
            pe.wait_ge(prep_read, 1)

            def quads(h, q, qp, hp):
                bank = (hp + qp) % 2
                wait(pe, adj_kept, Q * h + q - 1)
                for j in range(2):
                    for mi in range(2):
                        blockm = rawb[:, 2 * hp + j, bass.ds((2 * q + mi) * P, P)]
                        ins = nc.tensor.transpose(turned[:, bank, mi * NARROW + j * P:mi * NARROW + (j + 1) * P],
                                                  blockm, idb[:, :])
                ins.then_inc(quad_done, 1)

            def sum_step(bank, parts, q, slot, width, is_first, is_last, extra=None):
                for mi in range(2):
                    if extra:
                        extra(q, slot, mi, is_first and mi == 0)
                    for f in range(2):
                        for part in range(2):
                            ins = mm(bank[:, f, 0:width], parts[:, 2 * q + mi, part, f * P:(f + 1) * P],
                                     ring[:, slot, mi, 0:width], start=(is_first and mi == 0 and part == 0),
                                     stop=(is_last and mi == 1 and part == 1), skip_group_check=True)
                ins.then_inc(step_done, 1)

            def spread(c, cp, width):
                pe.wait_ge(slq_made, c + 1)
                if first(c):
                    pe.wait_ge(adj_kept, Q * HALVES)
                for b in range(width // P):
                    ins = mm(PA[cp][:, 0, b * P:(b + 1) * P], slq[:, b:b + 1].broadcast_to([P, P]), idf[:, :],
                             start=True, stop=True)
                ins.then_inc(slb_spread, 1)

            def products(blk, zt_count, b0, w):
                pe.wait_ge(zt_ready, zt_count)
                wait(pe, y_done, blk)
                for b in range(2):
                    for k in range(2):
                        ins = mm(prodv[:, b, :], zt[:, k, (b0 + b) * P:(b0 + b + 1) * P], w[:, k, :],
                                 start=(k == 0), stop=(k == 1))
                    ins.then_inc(prod_done, 1)

            pe.wait_ge(cast_done, 2)

            def step0(q, qp, last):
                quads(0, q, qp, 0)
            sweep(pe, step0, {1: lambda: None})

            def layer0(h, hp, more=True):
                if more:
                    pe.wait_ge(cast_done, 2 * h + 4)
                wait(pe, zt_ready, h - 1)
                if first(h):
                    pe.wait_ge(xs_ready, 1)

                def step(q, qp, last):
                    if more:
                        quads(h + 1, q, qp, 1 - hp)
                    pe.wait_ge(tile0, Q * h + q + 1)
                    sum_step(pairs[hp], xs, q, (hp + qp) % 2, NARROW, first(q), last)
                spots = {} if first(h) else {1: lambda: products(2 * (h - 1), h, 0, w02)}
                if not more:
                    spots[3] = lambda: spread(0, 0, WIDE)
                sweep(pe, step, spots)

            layer0(0, 0)
            layer0(1, 1)
            layer0(2, 0)
            with pe.Fori(1, (HALVES - 3) // 2) as i:
                layer0(2 * i + 1, 1)
                layer0(2 * i + 2, 0)
            layer0(HALVES - 2, 1)
            layer0(HALVES - 1, 0, more=False)

            def attention_products(blk, b):
                pe.wait_ge(p1c, blk + 1)
                for i, (src, w) in enumerate(((zt, wg), (ut, wsa))):
                    for k in range(2):
                        ins = mm(prodv[:, i, :], src[:, k, b * P:(b + 1) * P], w[:, k, :], start=(k == 0), stop=(k == 1))
                ins.then_inc(prod_done, 1)

            def gates_and_sums(c, cp, nblocks):
                pe.wait_ge(w_added, Q * (c + 1))
                pe.wait_ge(small_read, c + 1)
                for b in range(nblocks):
                    for mi in range(2):
                        mm(small[:, b:b + 1], wsum[:, cp, mi, b * P:(b + 1) * P], ones[:, 0:1],
                           start=(b == 0 and mi == 0), stop=False, skip_group_check=True)
                pe.wait_ge(zt_ready, ZT1 + c + 1)
                for b in range(nblocks):
                    for k in range(2):
                        ins = mm(small[:, 8 + 2 * b:10 + 2 * b], zt[:, k, b * P:(b + 1) * P], wgate[:, k, :],
                                 start=False, stop=False, skip_group_check=True)
                ins.then_inc(gates_done, 1)

            def first_attention_products(c):
                pe.wait_ge(ut_ready, c + 1)
                attention_products(4 * c, 0)

            def layer1(c, cp, width):
                slotted = (1 + cp) % 2
                if first(c):
                    pe.wait_ge(zt_ready, ZT1 - 1)
                    spots = {1: lambda: products(NB - 2, ZT1, 0, w02)}
                else:
                    spots = {0: lambda: gates_and_sums(c - 1, 1 - cp, 4), 1: lambda: first_attention_products(c - 1)}
                    for b in range(1, 4):
                        spots[b + 1] = lambda b=b: attention_products(4 * (c - 1) + b, b)
                if not (isinstance(c, int) and c == CH - 1):
                    nextw = NARROW if isinstance(c, int) and c == CH - 2 else WIDE
                    spots[4] = lambda old=spots.get(4, lambda: None): (old(), spread(c + 1, 1 - cp, nextw))

                def step(q, qp, last):
                    slot = (slotted + qp) % 2
                    if first(c):
                        pe.wait_ge(xs_ready, q + 2)
                    if first(q) and not first(c):
                        pe.wait_ge(zt_ready, ZT1 + c)
                    pe.wait_ge(tile_z, Q * c + q + 1)
                    for mi in range(2):
                        for f in range(2):
                            for part in range(2):
                                ins = mm(PZ[:, f, 0:width], xs[:, 2 * q + mi, part, f * P:(f + 1) * P],
                                         ring[:, slot, mi, 0:width], start=(first(q) and mi == 0 and part == 0),
                                         stop=(last and mi == 1 and part == 1), skip_group_check=True)
                    ins.then_inc(z_done, 1)
                    if first(q):
                        pe.wait_ge(slb_ready, c + 1)
                    pe.wait_ge(w_low, Q * c + q + 1)
                    for mi in range(2):
                        for f in range(2):
                            for i, (part, wpart) in enumerate(((1, 0), (0, 0), (0, 1))):
                                ins = mm(PA[cp][:, f, 0:width], xs[:, 2 * q + mi, part, f * P:(f + 1) * P],
                                         wr[:, slot, wpart, mi, 0:width], start=(first(q) and mi == 0 and i == 0),
                                         stop=(last and mi == 1 and i == 2), skip_group_check=True)
                    ins.then_inc(step_done, 1)
                sweep(pe, step, spots)

            chunks(pe, layer1)

            def layer2(c, cp, width):
                if first(c):
                    pe.wait_ge(zt_ready, ZT2)
                    spots = {0: lambda: gates_and_sums(CH - 1, 0, 2), 1: lambda: first_attention_products(CH - 1),
                             2: lambda: attention_products(4 * (CH - 1) + 1, 1)}
                else:
                    spots = {2: lambda: products(2 * NB + 4 * (c - 1), ZT2 + c, 0, w02),
                             4: lambda: products(2 * NB + 4 * (c - 1) + 2, ZT2 + c, 2, w02)}
                    pe.wait_ge(ut_ready, CH)
                    pe.wait_ge(zt_ready, ZT2 + c - 1)

                def step(q, qp, last):
                    if first(c):
                        pe.wait_ge(xs_ready, Q + q + 2)
                    pe.wait_ge(tile_z, Q * (CH + c) + q + 1)
                    own = xs2 if early[0] else xs
                    sum_step(pairs[1 - cp], own, q, (SW2 + cp + qp) % 2, width, first(q), last)
                early = [True]

                def past_early(old=spots.get(EARLY // 2, lambda: None)):
                    early[0] = False
                    old()
                spots[EARLY // 2] = past_early
                sweep(pe, step, spots)
                if first(c):
                    pe.wait_ge(w2_loaded, 32)
            chunks(pe, layer2)

            def layer3(c, cp, width):
                nb = width // P
                qsum = (small[:, 0:8], pairs[2][:, 0, 0:8])[cp]
                if first(c):
                    pe.wait_ge(small_read, CH + 1)
                    pe.wait_ge(ut_ready, CH)
                    pe.wait_ge(cols_pool, 10)
                    spots = {1: lambda: products(3 * NB - 2, ZT3, 0, w02)}
                else:
                    spots = {2: lambda: products(3 * NB + 4 * (c - 1), ZT3 + c, 0, w3),
                             4: lambda: products(3 * NB + 4 * (c - 1) + 2, ZT3 + c, 2, w3)}
                    pe.wait_ge(q_read, c)
                pe.wait_ge(zt_ready, ZT3 + c - 1)

                def extra(q, slot, mi, start):
                    for b in range(nb):
                        mm(qsum[:, 2 * b:2 * b + 2], ring[:, slot, mi, b * P:(b + 1) * P], rpart[:, 2 * q + mi, :],
                           start=(start and b == 0), stop=False, skip_group_check=True)

                def own():
                    for b in range(nb):
                        mm(qsum[:, 2 * b:2 * b + 2], idb[:, :], rpart[:, 4 * c + b, :], start=False, stop=False,
                           skip_group_check=True)
                        for f in range(2):
                            for part in range(2):
                                mm(pairs[cp][:, f, b * P:(b + 1) * P], xs[:, 4 * c + b, part, f * P:(f + 1) * P],
                                   idb[:, :], start=False, stop=False, skip_group_check=True)
                spots[5] = own

                def step(q, qp, last):
                    if first(c):
                        pe.wait_ge(xs_ready, 2 * Q + q + 2)
                    pe.wait_ge(tile_z, Q * (2 * CH + c) + q + 1)
                    sum_step(pairs[cp], xs, q, (SW3 + cp + qp) % 2, width, first(q), last, extra)
                sweep(pe, step, spots)
            chunks(pe, layer3)
            products(4 * NB - 2, ZT3 + CH, 0, w3)

        @block.vector
        def _(dve):
            v = nc.vector
            made = [0]

            def prep(ins):
                made[0] += 1
                ins.then_inc(prep_dve, 1)
                dve.wait_ge(prep_dve, made[0])

            dve.wait_ge(w_loaded, 16 * 17)
            dve.wait_ge(const_made, 12)
            for side in range(2):
                for k in range(2):
                    prep(v.scalar_tensor_tensor(out=t[:, 0, :], in0=wsa[:, k, :], scalar=1.0,
                                                in1=t_asa[:, side * D:(side + 1) * D], op0=ALU.mult, op1=ALU.mult,
                                                accum_out=vcol[:, 2 * side + k:2 * side + k + 1]))
            for i in range(4):
                prep(v.tensor_scalar(t_diag[:, i * P:(i + 1) * P], idf[:, :], vcol[:, i:i + 1], None, ALU.mult))
            dve.wait_ge(prep_pe, 1)
            prep(v.tensor_copy(t_w32t, pairs[0][:, 0, 0:D]))
            prep(v.tensor_scalar(t_b31, ones[:, :], b31c[:, :], None, ALU.mult))
            prep(v.tensor_copy(vrow[:, :, :], prodv))
            dve.wait_ge(prep_pe, 2)
            prep(v.tensor_copy(w3[:, :, :], pairs[0][:, 1, :].rearrange("p (k d) -> p k d", k=2)))
            prep(v.tensor_tensor(bias3[:, :], pairs[1][:, 0, 0:D], bias3[:, :], ALU.add))
            v.tensor_scalar(bias3[:, :], bias3[:, :], XS / US, None, ALU.mult)
            v.tensor_scalar(biasg[:, :], biasg[:, :], XS, None, ALU.mult).then_inc(prep_read, 1)
            prep(v.scalar_tensor_tensor(out=t[:, 0, :], in0=vrow[:, 1, :], scalar=1.0, in1=vrow[:, 1, :],
                                        op0=ALU.mult, op1=ALU.mult, accum_out=kcol[:, 0:1]))
            dve.wait_ge(x_loaded, 48)
            assert made[0] == 14
            prep(v.tensor_reduce(mxc[:, 0:1], x32[:, :, :].rearrange("p b d -> p (b d)"), AX.X, ALU.max,
                                 apply_absolute_value=True))
            dve.wait_ge(prep_pool, 2)
            prep(v.tensor_scalar(mxc[:, 1:2], mxc[:, 1:2], 2.0 ** -100, None, ALU.max))
            prep(v.tensor_scalar(mxc[:, 2:3].bitcast(I32), mxc[:, 1:2].bitcast(I32), EXPONENT, None, ALU.bitwise_and))
            prep(v.reciprocal(mxc[:, 3:4], mxc[:, 2:3]))
            prep(v.tensor_scalar(mxc[:, 3:4], mxc[:, 3:4], 2.0 ** 14, None, ALU.mult))
            prep(v.tensor_scalar(kcol[:, 2:3], kcol[:, 1:2], -0.16, LN_WS, ALU.mult, ALU.add))
            prep(v.tensor_scalar(kcol[:, 3:4], kcol[:, 1:2], 0.16, -LN_WS, ALU.mult, ALU.add))
            prep(v.tensor_scalar(xs[:, :, 0, :], x32[:, :, :], mxc[:, 3:4], None, ALU.mult))
            v.scalar_tensor_tensor(out=xs[:, :, 1, :], in0=x32[:, :, :], scalar=mxc[:, 3:4], in1=xs[:, :, 0, :],
                                   op0=ALU.mult, op1=ALU.subtract).then_inc(xs_ready, 1)
            prep(v.tensor_scalar(bias02[:, :], bias02[:, :], mxc[:, 3:4], None, ALU.mult))
            prep(v.tensor_scalar(mxc[:, 2:3], mxc[:, 2:3], 2.0 ** -14, None, ALU.mult))
            prep(v.tensor_scalar(sxcol[:, :], onecol[:, :], mxc[:, 2:3], None, ALU.mult))

            def keep(h, q, qp, hp):
                dve.wait_ge(quad_done, Q * h + q + 1)
                v.tensor_copy(adj_t[:, bass.ds(2 * q, 2), bass.ds(h * NARROW, NARROW)],
                              turned[:, (hp + qp) % 2, 0:WIDE].rearrange("p (m n) -> p m n", m=2)).then_inc(adj_kept, 1)

            def variances(blk, n):
                for b in range(2):
                    wait_apart(dve, y_done, blk + b + 1)
                    v.bn_stats(st[:, b, :], x32[:, n + b, :]).then_inc(st_done, 1)
                for b in range(2):
                    wait_apart(dve, st_done, blk + b + 1)
                    v.bn_aggr(mv[:, b, :], st[:, b, :]).then_inc(mv_done, 1)

            def scale_rows(n, pair):
                dve.wait_ge(rstd_done, pair + 1)
                for b in range(2):
                    v.tensor_scalar(x32[:, n + b, :], x32[:, n + b, :], mv[:, b, 0:1], rstd[:, b:b + 1],
                                    ALU.subtract, ALU.mult).then_inc(x_done, 1)

            def residual(blk, n, bias, col_a, col_b, affs=None):
                affs = blk if affs is None else affs
                dve.wait_ge(prod_done, blk + 2)
                for b in range(2):
                    v.scalar_tensor_tensor(out=prodv[:, b, :], in0=bias, scalar=col_a[:, bass.ds(n + b, 1)],
                                           in1=prodv[:, b, :], op0=ALU.mult, op1=ALU.add).then_inc(aff_done, 1)
                for b in range(2):
                    dve.wait_ge(aff_done, affs + b + 1)
                    v.scalar_tensor_tensor(out=x32[:, n + b, :], in0=prodv[:, b, :], scalar=col_b[:, bass.ds(n + b, 1)],
                                           in1=x32[:, n + b, :], op0=ALU.mult, op1=ALU.add).then_inc(y_done, 1)

            def finish(blk, n, pair, bias, col_a, col_b, affs=None):
                residual(blk, n, bias, col_a, col_b, affs)
                variances(blk, n)
                scale_rows(n, pair)

            def dots0(h):
                for b in range(2):
                    dve.wait_ge(x_done, 2 * h + b + 1)
                    for side, (sign, col) in enumerate(((1.0, slc), (-1.0, nsr))):
                        if b == 1:
                            dve.wait_ge(dot_done, 4 * h + side + 1)
                        v.scalar_tensor_tensor(out=t[:, side, :], in0=x32[:, 2 * h + b, :], scalar=sign,
                                               in1=vrow[:, side, :], op0=ALU.mult, op1=ALU.mult,
                                               accum_out=col[:, bass.ds(2 * h + b, 1)]).then_inc(dot_done, 1)

            def stages0(h, at):
                return {at: lambda: residual(2 * h, 2 * h, bias02[:, :], onecol, sxcol), at + 1: lambda: variances(2 * h, 2 * h),
                        at + 2: lambda: scale_rows(2 * h, h), at + 3: lambda: dots0(h)}

            def keep0(q, qp, last):
                keep(0, q, qp, 0)
            sweep(dve, keep0, {})

            def layer0(h, hp):
                def step(q, qp, last):
                    keep(h + 1, q, qp, 1 - hp)
                sweep(dve, step, {} if first(h) else stages0(h - 1, 2))
            layer0(0, 0)
            with dve.Fori(0, (HALVES - 3) // 2) as i:
                layer0(2 * i + 1, 1)
                layer0(2 * i + 2, 0)
            layer0(HALVES - 2, 1)

            def x_low(dest, q, base, scale):
                two = bass.ds(2 * q, 2)
                dve.wait_ge(hi_done, base + q + 1)
                v.scalar_tensor_tensor(out=dest[:, two, 1, :], in0=x32[:, two, :], scalar=scale, in1=dest[:, two, 0, :],
                                       op0=ALU.mult, op1=ALU.subtract).then_inc(xs_ready, 1)

            def scaled_parts(dest, col, q, his, base, ready):
                for mi in range(2):
                    v.tensor_scalar(dest[:, 2 * q + mi, 0, :], x32[:, 2 * q + mi, :], col[:, bass.ds(2 * q + mi, 1)], None,
                                    ALU.mult).then_inc(his, 1)
                for mi in range(2):
                    dve.wait_ge(his, base + 2 * q + mi + 1)
                    ins = v.scalar_tensor_tensor(out=dest[:, 2 * q + mi, 1, :], in0=x32[:, 2 * q + mi, :],
                                                 scalar=col[:, bass.ds(2 * q + mi, 1)],
                                                 in1=dest[:, 2 * q + mi, 0, :], op0=ALU.mult, op1=ALU.subtract)
                ins.then_inc(ready, 1)

            def stage_left(c, nblocks):
                wait(dve, slb_spread, c)
                v.tensor_copy(slq[:, 0:nblocks], slc[:, bass.ds(4 * c, nblocks)]).then_inc(slq_made, 1)

            dve.wait_ge(dot_done, 8)
            v.tensor_copy(slq[:, 0:4], slc[:, 0:4]).then_inc(slq_made, 1)

            def final_step(q, qp, last):
                if not (isinstance(q, int) and q < 2):
                    x_low(xs, q - 2, 0, XS)
            stages = stages0(HALVES - 2, 2)
            stages.update({1: lambda: None})
            sweep(dve, final_step, stages)
            dve.wait_ge(dot_done, 2 * (NB - 2))
            v.tensor_scalar(wbias[:, 0:NB - 2], nsr[:, 0:NB - 2], kcol[:, 2:3], None, ALU.add).then_inc(cols_dve, 1)
            x_low(xs, Q - 2, 0, XS)

            def last_columns():
                dve.wait_ge(dot_done, 2 * NB)
                v.tensor_scalar(wbias[:, NB - 2:NB], nsr[:, NB - 2:NB], kcol[:, 2:3], None, ALU.add).then_inc(cols_dve, 1)
                v.memset(sm[:, :], 0.0).then_inc(p1c, 1)
                v.memset(den[:, :], 0.0).then_inc(small_read, 1)

            NCOL = 6

            def attention_columns(c, nblocks):
                k = [0]

                def link(ins):
                    k[0] += 1
                    ins.then_inc(chunk_cols, 1)
                    dve.wait_ge(chunk_cols, NCOL * c + k[0])
                dve.wait_ge(wx_loaded, 32)
                dve.wait_ge(cols_act, 3)
                for b in range(nblocks):
                    for side in range(2):
                        if b > 0:
                            dve.wait_ge(xab_dots, 8 * c + 2 * b + side - 1)
                        v.scalar_tensor_tensor(out=t[:, side, :], in0=x32[:, 4 * c + b, :], scalar=1.0,
                                               in1=vrow[:, side, :], op0=ALU.mult, op1=ALU.mult,
                                               accum_out=xab[:, b, side:side + 1]).then_inc(xab_dots, 1)
                dve.wait_ge(xab_dots, 8 * c + 2 * nblocks)
                n4 = slice(0, nblocks)
                link(v.tensor_tensor(xab[:, n4, :], xab[:, n4, :], bab[:, :].unsqueeze(1).broadcast_to([P, nblocks, 2]), ALU.add))
                dve.wait_ge(gates_done, c + 1)
                v.tensor_copy(sm[:, 0:nblocks], small[:, 0:nblocks])
                v.tensor_copy(sm[:, 4:4 + 2 * nblocks], small[:, 8:8 + 2 * nblocks]).then_inc(small_read, 1)
                dve.wait_ge(small_read, c + 2)
                v.scalar_tensor_tensor(out=gate[:, n4, :], in0=sm[:, 4:4 + 2 * nblocks].rearrange("p (b s) -> p b s", s=2),
                                       scalar=1.0 / XS, in1=xab[:, n4, :], op0=ALU.mult, op1=ALU.add).then_inc(gate_pre, 1)
                four = bass.ds(4 * c, nblocks)
                link(v.tensor_tensor(den[:, n4], sm[:, n4], ccol[:, four], ALU.mult))
                link(v.tensor_scalar(den[:, n4], den[:, n4], 1e-5, None, ALU.add))
                link(v.reciprocal(den[:, n4], den[:, n4]))
                link(v.tensor_tensor(den[:, n4], den[:, n4], ccol[:, four], ALU.mult))
                dve.wait_ge(gate_tanh, c + 1)
                link(v.tensor_scalar(coef[:, n4, :], gate[:, n4, :], 1.0, 0.5 / XS, ALU.add, ALU.mult))
                v.tensor_tensor(coef[:, n4, 0], coef[:, n4, 0], den[:, n4], ALU.mult).then_inc(q_col, 1)
                assert k[0] == NCOL
                dve.wait_ge(q_col, c + 1)

            def mix(blk, b):
                dve.wait_ge(prod_done, NB + blk + 1)
                v.tensor_tensor(t[:, b % 2, :], prodv[:, 0, :], biasg[:, :], ALU.add).then_inc(p1a, 1)
                dve.wait_ge(p1a, blk + 1)
                v.tensor_scalar(t[:, b % 2, :], t[:, b % 2, :], coef[:, b, 1:2], None, ALU.mult).then_inc(p1b, 1)
                dve.wait_ge(p1b, blk + 1)
                v.scalar_tensor_tensor(out=t[:, b % 2, :], in0=prodv[:, 1, :], scalar=coef[:, b, 0:1], in1=t[:, b % 2, :],
                                       op0=ALU.mult, op1=ALU.add).then_inc(p1c, 1)

            def finish1(c, b0):
                for b in range(2):
                    dve.wait_ge(th_done, 4 * c + b0 + b + 1)
                    v.scalar_tensor_tensor(out=x32[:, 4 * c + b0 + b, :], in0=t[:, b, :], scalar=0.5,
                                           in1=x32[:, 4 * c + b0 + b, :], op0=ALU.mult, op1=ALU.add).then_inc(y_done, 1)
                variances(NB + 4 * c + b0, 4 * c + b0)
                scale_rows(4 * c + b0, HALVES + 2 * c + b0 // 2)

            def layer1(c, cp, width):
                slotted = (1 + cp) % 2

                def low(q, slot):
                    dve.wait_ge(w_high, Q * c + q + 1)
                    v.tensor_tensor(wr[:, slot, 1, :, 0:width], wf[:, slot, :, 0:width], wr[:, slot, 0, :, 0:width],
                                    ALU.subtract).then_inc(w_low, 1)

                def step(q, qp, last):
                    slot = (slotted + qp) % 2
                    dve.wait_ge(exp_done, Q * c + q + 1)
                    if first(c) and last:
                        dve.wait_ge(cols_act, 2)
                    for mi in range(2):
                        ins = v.scalar_tensor_tensor(out=wf[:, slot, mi, 0:width], in0=wf[:, slot, mi, 0:width],
                                                     scalar=wcap[:, bass.ds(2 * q + mi, 1)],
                                                     in1=adj_t[:, 2 * q + mi, bass.ds(c * WIDE, width)],
                                                     op0=ALU.min, op1=ALU.mult)
                    ins.then_inc(masked, 1)
                    if not first(q):
                        low(q - 1, 1 - slot)
                    if isinstance(c, int) and c == CH - 2 and first(q):
                        x_low(xs2, 0, Q, XS)

                def early_pair(j):
                    x_low(xs2, 2 * j + 1, Q, XS)
                    x_low(xs2, 2 * j + 2, Q, XS)

                if first(c):
                    dve.wait_ge(cols_act, 1)
                    h = HALVES - 1
                    spots = {2: lambda: (residual(2 * h, 2 * h, bias02[:, :], onecol, sxcol), variances(2 * h, 2 * h)),
                             3: lambda: (scale_rows(2 * h, h), dots0(h), last_columns(), stage_left(1, 4)),
                             5: lambda: x_low(xs, Q - 1, 0, XS)}
                else:
                    spots = {1: lambda: attention_columns(c - 1, 4), 2: lambda: mix(4 * (c - 1), 0),
                             3: lambda: mix(4 * (c - 1) + 1, 1),
                             4: lambda: (finish1(c - 1, 0), mix(4 * (c - 1) + 2, 2)), 5: lambda: mix(4 * (c - 1) + 3, 3)}
                    if not (isinstance(c, int) and c == CH - 1):
                        nextb = 2 if isinstance(c, int) and c == CH - 2 else 4
                        spots[3] = lambda old=spots[3]: (old(), stage_left(c + 1, nextb))
                    if isinstance(c, int) and c == CH - 2:
                        spots[0] = lambda: early_pair(0)
                        for j in (1, 2):
                            spots[j + 2] = lambda j=j, old=spots[j + 2]: (old(), early_pair(j))
                sweep(dve, step, spots)
                low(Q - 1, slotted)
                if not first(c):
                    finish1(c - 1, 2)
            chunks(dve, layer1)

            with dve.Fori(EARLY, Q - 1) as q:
                x_low(xs, q, Q, XS)
            attention_columns(CH - 1, 2)
            mix(4 * (CH - 1), 0)
            mix(4 * (CH - 1) + 1, 1)
            finish1(CH - 1, 0)
            x_low(xs, Q - 1, Q, XS)
            dve.wait_ge(tile_z, Q * CH)
            v.tensor_reduce(degb[:, :], degp[:, :].rearrange("p (c m) -> p m c", c=CH), AX.X, ALU.add).then_inc(cols_dve, 1)
            dve.wait_ge(cols_dve, 3)
            v.tensor_tensor(degb[:, :], degb[:, :], pad[:, :], ALU.add).then_inc(cols_dve, 1)
            dve.wait_ge(cols_dve, 4)
            v.reciprocal(degb[:, :], degb[:, :]).then_inc(cols_dve, 1)
            dve.wait_ge(cols_dve, 5)
            v.tensor_scalar(degb[:, :], degb[:, :], 1.0 / XS, None, ALU.mult).then_inc(cols_dve, 1)
            dve.wait_ge(cols_dve, 6)
            dve.wait_ge(w2_loaded, 32)
            v.tensor_scalar(bias02[:, :], bias02[:, :], XS, None, ALU.mult).then_inc(q_read, 1)
            dve.wait_ge(q_read, 1)

            def finish_chunk(L, c, bias, col_a, col_b):
                for b0 in (0, 2):
                    finish(L * NB + 4 * c + b0, 4 * c + b0, L * HALVES + 2 * c + b0 // 2, bias, col_a, col_b,
                           (L - 1) * NB + 4 * c + b0)

            def parts3(q):
                scaled_parts(xs, r3x, q, hi_done, 2 * Q, xs_ready)

            with dve.Fori(0, 4) as c:
                finish_chunk(2, c, bias02[:, :], rowsum, degb)
            dve.wait_ge(x_done, 2 * NB + 16)
            dve.wait_ge(cols_pool, 10)
            with dve.Fori(0, EARLY) as q:
                parts3(q)
            with dve.Fori(4, CH - 1) as c:
                finish_chunk(2, c, bias02[:, :], rowsum, degb)
            dve.wait_ge(x_done, 3 * NB - 2)
            with dve.Fori(EARLY, Q - 1) as q:
                dve.wait_ge(step_done, Q * (SW3 - 1) + q + 1)
                parts3(q)
            finish(3 * NB - 2, NB - 2, 3 * HALVES - 1, bias02[:, :], rowsum, degb, 2 * NB - 2)
            dve.wait_ge(x_done, 3 * NB)
            dve.wait_ge(step_done, Q * SW3)
            scaled_parts(xs, r3x, Q - 1, hi_done, 2 * Q, xs_ready)

            def q_column(c, cp, nblocks):
                dve.wait_ge(step_done, Q * (SW3 + c + 1))
                qsum = (small[:, 0:2 * nblocks], pairs[2][:, 0, 0:2 * nblocks])[cp]
                v.tensor_copy(qs_sb[:, 0:2 * nblocks], qsum).then_inc(q_read, 1)
                dve.wait_ge(q_read, c + 2)
                qv = qs_sb[:, 0:2 * nblocks].rearrange("p (b s) -> p b s", s=2)
                v.tensor_tensor(qcol[:, bass.ds(4 * c, nblocks)], qv[:, :, 0], qv[:, :, 1], ALU.add).then_inc(q_col, 1)
                dve.wait_ge(q_col, CH + c + 1)

            with dve.Fori(0, 3) as i:
                for cp in range(2):
                    q_column(2 * i + cp, cp, 4)
                    finish_chunk(3, 2 * i + cp, bias3[:, :], qcol, r3b)
            q_column(CH - 1, 0, 2)
            finish(4 * NB - 2, NB - 2, 4 * HALVES - 1, bias3[:, :], qcol, r3b, 3 * NB - 2)


_INS = ['x', 'adj', 'L0_gnn_W', 'L0_gnn_b', 'L1_gnn_W_sa', 'L1_gnn_a_sa', 'L1_gnn_W_gcnb', 'L1_gnn_b_gcnb',
        'L1_gnn_Wa', 'L1_gnn_ba', 'L1_gnn_Wb', 'L1_gnn_bb', 'L2_gnn_W', 'L2_gnn_b',
        'L3_gnn_W1', 'L3_gnn_b1', 'L3_gnn_W2', 'L3_gnn_b2']


def kernel(**inputs):
    import numpy as _np
    import concourse.bacc as _bacc
    from concourse import mybir as _mybir
    from concourse.bass_utils import run_bass_kernel_spmd as _run

    nc = _bacc.Bacc("TRN2", target_bir_lowering=False, num_devices=1, dynamic_dma_scratch_size=256)
    arrays, args = {}, []
    for name in _INS:
        a = _np.ascontiguousarray(inputs[name])
        arrays[f"in_{name}_dram"] = a
        args.append(nc.dram_tensor(f"in_{name}_dram", a.shape, _mybir.dt.from_np(a.dtype), kind="ExternalInput").ap())
    shape = tuple(inputs['x'].shape)
    args.append(nc.dram_tensor("out_0_dram", shape, _mybir.dt.float32, kind="ExternalOutput").ap())
    four_graph_layers(nc, *args)
    r = _run(nc, [arrays], core_ids=[0])
    return r.results[0]["out_0_dram"]
```

```python
import concourse.bass as bass
from concourse import mybir
from contextlib import ExitStack
import math


def four_graph_layers(nc, x, adj, w0, b0, w_sa, a_sa, w_gcn, b_gcn, wa, ba, wb, bb, w2, b2,
                      w31, b31, w32, b32, out):
    F32, BF16, F16 = mybir.dt.float32, mybir.dt.bfloat16, mybir.dt.float16
    U8, I32 = mybir.dt.uint8, mybir.dt.int32
    ALU, ACT, AX = mybir.AluOpType, mybir.ActivationFunctionType, mybir.AxisListType

    P = 128
    N, D = x.shape
    NB = (N + P - 1) // P
    NP = NB * P
    TAIL = N - (NB - 1) * P
    TAIL_A = TAIL // 16 * 16
    Q = NB // 2
    PAIRS = (Q - 1) // 2
    WIDE, NARROW = 512, 256
    CH = NP // WIDE + 1
    HALVES = NP // NARROW
    MID = Q // 2
    HEADS, DPH = w0.shape[0], w0.shape[2]
    EPS = 1e-5
    XS = 2.0 ** 11
    LN_WS = 15 * math.log(2.0)
    CUTS = (0, NB // 3, NB * 2 // 3, NB - 1)
    AHEAD = Q - 3
    LOWS = 4
    GROUPS = (0, NB - 8, NB - 4, NB)
    EARLY = 7
    EXPONENT = 0x7F800000
    assert D == 2 * P and NB % 2 == 0 and PAIRS == 6 and (CH - 1) * WIDE + NARROW == NP

    SW1 = CH
    SW2 = SW1 + CH
    SW3 = SW2 + CH
    ZT1 = CH
    ZT2 = ZT1 + CH
    ZT3 = ZT2 + CH

    ctx = ExitStack()
    with ctx:
        def sb(name, shape, dt):
            return ctx.enter_context(nc.sbuf_tensor(name, shape, dt))

        def sem(name):
            return ctx.enter_context(nc.semaphore(name))

        adj_t = sb("adj_t", [P, NB, NP], U8)
        x32 = sb("x32", [P, NB, D], F32)
        xs = sb("xs", [P, NB, 2, D], F16)
        zone = sb("zone", [P, 2 * NP * 2 * 2], BF16)
        raw = zone[:, 0:4 * NP].bitcast(F32).rearrange("p (s n) -> p s n", s=2)
        rawb = zone[:, 4 * NP:8 * NP].rearrange("p (s n) -> p s n", s=4)
        wf = zone[:, 0:8 * WIDE].bitcast(F32).rearrange("p (s m n) -> p s m n", s=2, m=2)
        wsum = zone[:, 8 * WIDE:16 * WIDE].bitcast(F32).rearrange("p (s m n) -> p s m n", s=2, m=2)
        wr = zone[:, 16 * WIDE:24 * WIDE].bitcast(F16).rearrange("p (s t m n) -> p s t m n", s=2, t=2, m=2)
        t1 = zone[:, 8 * NP - 8 * D:8 * NP].bitcast(F32).rearrange("p (b d) -> p b d", b=4)
        qacc = zone[:, 0:2 * NP].bitcast(F32)
        xs2 = zone[:, 24 * WIDE:24 * WIDE + EARLY * 4 * D].bitcast(F16).rearrange("p (m t d) -> p m t d", t=2, d=D)
        w02 = sb("w02", [P, 2, D], F32)
        wg = sb("wg", [P, 2, D], F32)
        wgate = sb("wgate", [P, 2, 2], F32)
        wsa = sb("wsa", [P, 2, D], F32)
        w3 = sb("w3", [P, 2, D], F32)
        bias02 = sb("bias02", [P, D], F32)
        biasg = sb("biasg", [P, D], F32)
        bias3 = sb("bias3", [P, D], F32)
        vrow = sb("vrow", [P, 2, D], F32)
        idf = sb("idf", [P, P], F32)
        idb = sb("idb", [P, P], BF16)
        ones = sb("ones", [P, P], F32)
        mhalf = sb("mhalf", [P, NB], F32)
        pad = sb("pad", [P, NB], F32)
        zt = sb("zt", [P, 2, WIDE], F32)
        ut = sb("ut", [P, 2, WIDE], F32)
        slb = sb("slb", [P, 2, WIDE], F32)
        ring = sb("ring", [P, 2, 2, WIDE], BF16)
        t = sb("t", [P, 2, D], F32)
        columns = sb("columns", [P, 11, NB], F32)
        (rowsum, slc, nsr, wcap, wbias, ccol, degb, r3, r3x, r3b, qcol) = (columns[:, i, :] for i in range(11))
        sxcol, onecol = degb, qcol
        degp = sb("degp", [P, CH * NB], F32)
        little = sb("little", [P, 120], F32)
        taken = [0]

        def piece(*shape):
            size = 1
            for s in shape:
                size *= s
            taken[0] += size
            ap = little[:, taken[0] - size:taken[0]]
            return ap if len(shape) == 1 else ap.rearrange("p (a b) -> p a b", a=shape[0])
        vcol, kcol, mxc, mxp, bab, b31c = piece(4), piece(4), piece(4), piece(3), piece(2), piece(1)
        st, mv, ve, rstd = piece(2, 6), piece(4, 2), piece(2), piece(4)
        sm, den, slq = piece(12), piece(4), piece(4)
        xab, gate, coef = piece(4, 2), piece(4, 2), piece(4, 2)
        half, eps = piece(1), piece(2)

        pairs = [ctx.enter_context(nc.psum_tensor(f"sum{i}", [P, 2, WIDE], F32)) for i in range(3)]
        prod = ctx.enter_context(nc.psum_tensor("prod", [P, WIDE], F32))
        small = ctx.enter_context(nc.psum_tensor("small", [P, WIDE], F32))
        turned = pairs[2][:, :, :].bitcast(BF16)
        PZ = pairs[1]
        PA = (pairs[2], pairs[0])
        prodv = prod[:, :].rearrange("p (b d) -> p b d", b=2)

        t_asa = zt[:, 0, :]
        t_diag = ut[:, 0, :]
        t_w31 = ut[:, 1, 0:D]
        t_w32 = ut[:, 1, D:2 * D].rearrange("p (k h) -> p k h", k=2)
        t_w32t = slb[:, 0, 0:D]
        t_b31 = slb[:, 0, D:D + P]

        x_loaded = [sem("x_loaded0"), sem("x_loaded1"), sem("x_loaded2")]
        w_loaded, late_loaded, w2_loaded, wx_loaded = sem("w_loaded"), sem("late_loaded"), sem("w2_loaded"), sem("wx_loaded")
        raw_loaded = [sem("raw_loaded0"), sem("raw_loaded1")]
        out_stored = sem("out_stored")
        const_made = sem("const_made")
        prep_dve, prep_pe, prep_read, prep_pool = sem("prep_dve"), sem("prep_pe"), sem("prep_read"), sem("prep_pool")
        cast_done, quad_done, adj_kept = sem("cast_done"), sem("quad_done"), sem("adj_kept")
        tile0, tile_z = sem("tile0"), sem("tile_z")
        exp_done, masked, w_high, w_low, w_added = (sem("exp_done"), sem("masked"), sem("w_high"), sem("w_low"),
                                                    sem("w_added"))
        step_done, z_done = sem("step_done"), sem("z_done")
        zt_ready, ut_ready = sem("zt_ready"), sem("ut_ready")
        prod_done, aff_done, y_done, st_done, mv_done = (sem("prod_done"), sem("aff_done"), sem("y_done"),
                                                         sem("st_done"), sem("mv_done"))
        ve_done, rstd_done, x_done = sem("ve_done"), sem("rstd_done"), sem("x_done")
        dot_done = sem("dot_done")
        hi_done, xs_ready = sem("hi_done"), sem("xs_ready")
        cols_dve, cols_act, cols_pool = sem("cols_dve"), sem("cols_act"), sem("cols_pool")
        slq_made, slb_spread, slb_ready = sem("slq_made"), sem("slb_spread"), sem("slb_ready")
        gates_done, small_read, gate_pre, gate_tanh, chunk_cols = (sem("gates_done"), sem("small_read"), sem("gate_pre"),
                                                                   sem("gate_tanh"), sem("chunk_cols"))
        p1a, p1b, p1c, th_done = sem("p1a"), sem("p1b"), sem("p1c"), sem("th_done")
        sums_made, diag_added = sem("sums_made"), sem("diag_added")
        q_read, q_col, q_made, q_summed, q_added = (sem("q_read"), sem("q_col"), sem("q_made"), sem("q_summed"),
                                                    sem("q_added"))
        waits_apart, xab_dots = sem("waits_apart"), sem("xab_dots")

        block = ctx.enter_context(nc.Block())

        def wait(eng, s, value):
            if isinstance(value, int) and value <= 0:
                return
            eng.wait_ge(s, value)

        def wait_apart(eng, s, value):
            eng.wait_ge(s, value)
            eng.sem_inc(waits_apart, 1)

        def sweep(eng, step, spots, mids={}):
            step(0, 0, False)
            j = 0
            while j < PAIRS:
                if j in spots:
                    spots[j]()
                k = j + 1
                while k < PAIRS - 1 and k not in spots and j not in mids:
                    k += 1
                if k - j > 1:
                    with eng.Fori(j, k) as r:
                        step(2 * r + 1, 1, False)
                        step(2 * r + 2, 0, False)
                else:
                    step(2 * j + 1, 1, False)
                    if j in mids:
                        mids[j]()
                    step(2 * j + 2, 0, j == PAIRS - 1)
                j = k

        def chunks(eng, body):
            body(0, 0, WIDE)
            with eng.Fori(0, 2) as i:
                body(2 * i + 1, 1, WIDE)
                body(2 * i + 2, 0, WIDE)
            body(5, 1, WIDE)
            body(6, 0, NARROW)

        def two_quads(q, late):
            if isinstance(q, int) and q == MID:
                return (0, Q - 1, 0), (1, 0, 0)
            if late:
                return (1, 2 * q - Q, 1), (1, 2 * q - Q + 1, 0)
            return (0, 2 * q, 0), (0, 2 * q + 1, 1)

        def layer0_spots(late, spots):
            def past(old=spots.get(MID // 2, lambda: None)):
                late[0] = True
                old()
            spots = dict(spots)
            spots[MID // 2] = past
            spots.setdefault(MID // 2 - 1, lambda: None)
            return spots

        def targets0(k):
            return (0, NARROW) if first(k) else (k * WIDE - NARROW, WIDE)

        def first(c):
            return isinstance(c, int) and c == 0

        @block.sync
        def _(sp):
            for i in range(3):
                lo, hi = CUTS[i], CUTS[i + 1]
                sp.dma_start(x32[:, lo:hi, :], x[lo * P:hi * P, :].rearrange("(b p) d -> p b d", p=P)).then_inc(x_loaded[i], 16)
            sp.wait_ge(const_made, 2)
            sp.dma_start(x32[0:TAIL_A, NB - 1, :], x[(NB - 1) * P:(NB - 1) * P + TAIL_A, :]).then_inc(x_loaded[2], 16)
            sp.dma_start(x32[TAIL_A:TAIL, NB - 1, :], x[(NB - 1) * P + TAIL_A:N, :]).then_inc(x_loaded[2], 16)
            sp.dma_start(raw[:, 0, 0:N], adj[0:P, :]).then_inc(raw_loaded[0], 16)
            sp.dma_start(raw[:, 1, 0:N], adj[P:2 * P, :]).then_inc(raw_loaded[1], 16)
            def row_pair(h):
                for s in range(2):
                    sp.wait_ge(cast_done, 2 * h - 1 + s)
                    sp.dma_start(raw[:, s, 0:N], adj[bass.ds((2 * h + s) * P, P), :]).then_inc(raw_loaded[s], 16)
            row_pair(1)
            for k in range(2):
                sp.dma_start(w02[:, k, :].rearrange("p (h e) -> p h e", h=HEADS),
                              w0[:, k * P:(k + 1) * P, :].rearrange("h p e -> p h e")).then_inc(w_loaded, 16)
            sp.dma_start(wsa[:, :, :], w_sa.rearrange("(k p) o -> p k o", p=P)).then_inc(w_loaded, 16)
            sp.dma_start(t_asa, a_sa[0, :].partition_broadcast(P)).then_inc(w_loaded, 16)
            sp.dma_start(t_w31, w31).then_inc(w_loaded, 16)
            sp.dma_start(t_w32, w32.rearrange("(k p) h -> p k h", p=P)).then_inc(w_loaded, 16)
            sp.dma_start(b31c[:, :], b31.rearrange("(p o) -> p o", o=1)).then_inc(w_loaded, 16)
            sp.dma_start(bias02[:, :], b0.rearrange("h e -> (h e)").partition_broadcast(P)).then_inc(late_loaded, 16)
            sp.dma_start(bias3[:, :], b32.partition_broadcast(P)).then_inc(late_loaded, 16)
            sp.dma_start(biasg[:, :], b_gcn.partition_broadcast(P)).then_inc(late_loaded, 16)
            sp.dma_start(wg[:, :, :], w_gcn.rearrange("(k p) o -> p k o", p=P)).then_inc(late_loaded, 16)
            sp.dma_start(bab[:, 0:1], ba.partition_broadcast(P)).then_inc(late_loaded, 16)
            sp.dma_start(bab[:, 1:2], bb.partition_broadcast(P)).then_inc(late_loaded, 16)
            for k in range(2):
                sp.dma_start(wgate[:, k, 0:1], wa[0, k * P:(k + 1) * P].rearrange("(p o) -> p o", o=1)).then_inc(late_loaded, 16)
                sp.dma_start(wgate[:, k, 1:2], wb[0, k * P:(k + 1) * P].rearrange("(p o) -> p o", o=1)).then_inc(late_loaded, 16)
            with sp.Fori(2, HALVES - 1) as h:
                row_pair(h)
            sp.wait_ge(cast_done, NB - 3)
            sp.dma_start(raw[:, 0, 0:N], adj[(NB - 2) * P:(NB - 1) * P, :]).then_inc(raw_loaded[0], 16)
            sp.wait_ge(cast_done, NB - 2)
            sp.dma_start(raw[0:TAIL_A, 1, 0:N], adj[(NB - 1) * P:(NB - 1) * P + TAIL_A, :]).then_inc(raw_loaded[1], 16)
            sp.dma_start(raw[TAIL_A:TAIL, 1, 0:N], adj[(NB - 1) * P + TAIL_A:N, :]).then_inc(raw_loaded[1], 16)
            sp.wait_ge(y_done, NB)
            sp.dma_start(w02[:, :, :], w2.rearrange("(k p) o -> p k o", p=P)).then_inc(w2_loaded, 16)
            sp.dma_start(bias02[:, :], b2.partition_broadcast(P)).then_inc(w2_loaded, 16)
            sp.wait_ge(dot_done, 2 * NB)
            sp.dma_start(vrow[:, 0, :], wa[0, D:2 * D].partition_broadcast(P)).then_inc(wx_loaded, 16)
            sp.dma_start(vrow[:, 1, :], wb[0, D:2 * D].partition_broadcast(P)).then_inc(wx_loaded, 16)
            with sp.Fori(0, CH - 1) as c:
                sp.wait_ge(x_done, 3 * NB + 4 * c + 4)
                sp.dma_start(out[bass.ds(c * WIDE, WIDE), :].rearrange("(b p) d -> p b d", p=P),
                             x32[:, bass.ds(4 * c, 4), :]).then_inc(out_stored, 16)
            sp.wait_ge(x_done, 4 * NB)
            sp.dma_start(out[(NB - 2) * P:(NB - 1) * P, :], x32[:, NB - 2, :]).then_inc(out_stored, 16)
            sp.dma_start(out[(NB - 1) * P:(NB - 1) * P + TAIL_A, :], x32[0:TAIL_A, NB - 1, :]).then_inc(out_stored, 16)
            sp.dma_start(out[(NB - 1) * P + TAIL_A:N, :], x32[TAIL_A:TAIL, NB - 1, :]).then_inc(out_stored, 16)
            sp.wait_ge(out_stored, 16 * (CH + 2))

        @block.gpsimd
        def _(pool):
            g = nc.gpsimd
            g.memset(raw[:, :, N:NP], 0.0).then_inc(const_made, 1)
            g.memset(x32[:, NB - 1, :], 0.0).then_inc(const_made, 1)
            g.memset(idf[:, :], 0.0).then_inc(const_made, 1)
            g.memset(pad[:, :], 0.0).then_inc(const_made, 1)
            pool.wait_ge(const_made, 4)
            g.affine_select(out=idf[:, :], in_=idf[:, :], compare_op=ALU.not_equal, fill=1.0, base=0,
                            pattern=[[-1, P]], channel_multiplier=1).then_inc(const_made, 1)
            g.affine_select(out=pad[:, :], in_=pad[:, :], compare_op=ALU.not_equal, fill=1.0, base=-N,
                            pattern=[[P, NB]], channel_multiplier=1).then_inc(const_made, 1)
            g.memset(ones[:, :], 1.0).then_inc(const_made, 1)
            g.memset(mhalf[:, :], -0.5).then_inc(const_made, 1)
            g.memset(half[:, :], 0.5).then_inc(const_made, 1)
            g.memset(eps[:, :], EPS).then_inc(const_made, 1)
            g.memset(onecol[:, :], 1.0).then_inc(const_made, 1)
            pool.wait_ge(const_made, 6)
            g.tensor_copy(idb[:, :], idf[:, :]).then_inc(const_made, 1)
            pool.wait_ge(const_made, 12)
            pool.wait_ge(prep_dve, 4)
            g.partition_all_reduce(mxc[:, 1:2], mxc[:, 0:1], P, bass.bass_isa.ReduceOp.max).then_inc(prep_pool, 1)
            pool.wait_ge(prep_dve, 22)
            g.tensor_tensor(out=kcol[:, 1:2], in0=kcol[:, 0:1], in1=half[:, :], op=ALU.pow).then_inc(prep_pool, 1)

            def inverse_deviation(pair, place=0):
                pool.wait_ge(mv_done, 2 * pair + 2)
                g.tensor_tensor(out=ve[:, :], in0=mv[:, 2 * place:2 * place + 2, 1], in1=eps[:, :], op=ALU.add).then_inc(ve_done, 1)
                pool.wait_ge(ve_done, pair + 1)
                g.tensor_tensor(out=rstd[:, 2 * place:2 * place + 2], in0=ve[:, :], in1=mhalf[:, 0:2], op=ALU.pow).then_inc(rstd_done, 1)

            with pool.Fori(0, HALVES - 2) as pair:
                inverse_deviation(pair)
            pool.wait_ge(cast_done, NB)
            n = [0]

            def column(ins):
                n[0] += 1
                ins.then_inc(cols_pool, 1)
                pool.wait_ge(cols_pool, n[0])
            column(g.tensor_scalar(r3, rowsum, 1.0, None, ALU.add))
            column(g.tensor_scalar(r3b, r3, 1e-30, None, ALU.max))
            column(g.tensor_tensor(out=r3x, in0=r3b, in1=mhalf[:, :], op=ALU.pow))
            column(g.tensor_scalar(r3b, r3, 0.0, None, ALU.is_gt))
            column(g.tensor_tensor(out=r3, in0=r3x, in1=r3b, op=ALU.mult))
            column(g.tensor_scalar(r3x, r3, XS, None, ALU.mult))
            column(g.tensor_scalar(r3b, r3, 1.0 / XS, None, ALU.mult))

            pool.wait_ge(tile0, Q * CH)
            g.memset(adj_t[:, :, N:NP], 0.0).then_inc(cols_pool, 1)
            pool.wait_ge(cols_pool, 8)
            def layer1(c, cp, width):
                def step(q, qp, last):
                    slot = (1 + cp + qp) % 2
                    wait_apart(pool, masked, Q * c + q + 1)
                    if first(q):
                        if not first(c):
                            wait_apart(pool, step_done, Q * (SW1 + c - 1) + 2)
                        g.tensor_copy(wsum[:, cp, :, 0:width], wf[:, slot, :, 0:width]).then_inc(w_added, 1)
                    else:
                        pool.wait_ge(w_added, Q * c + q)
                        g.tensor_tensor(out=wsum[:, cp, :, 0:width], in0=wsum[:, cp, :, 0:width],
                                        in1=wf[:, slot, :, 0:width], op=ALU.add).then_inc(w_added, 1)
                spots, mids = {}, {}
                if first(c):
                    spots = {1: lambda: inverse_deviation(HALVES - 2), 3: lambda: inverse_deviation(HALVES - 1)}
                else:
                    mids = {5: lambda: inverse_deviation(HALVES + 2 * (c - 1))}
                sweep(pool, step, spots, mids)
                if not first(c):
                    pool.wait_ge(rstd_done, HALVES + 2 * (c - 1) + 1)
                    inverse_deviation(HALVES + 2 * (c - 1) + 1, 1)
                pool.wait_ge(w_added, Q * (c + 1))
                g.tensor_tensor(out=wsum[:, cp, 0, 0:width], in0=wsum[:, cp, 0, 0:width], in1=wsum[:, cp, 1, 0:width],
                                op=ALU.add).then_inc(sums_made, 1)
            chunks(pool, layer1)
            with pool.Fori(2 * HALVES - 1, 4 * HALVES) as pair:
                inverse_deviation(pair)

        @block.scalar
        def _(act):
            a = nc.scalar
            def cast(h, hp, s, more=0):
                act.wait_ge(raw_loaded[s], 16 * (h + 1) + more)
                wait(act, quad_done, Q * (h - 1))
                a.activation(rawb[:, 2 * hp + s, :], raw[:, s, :], ACT.Copy,
                             accum_out=rowsum[:, bass.ds(2 * h + s, 1)]).then_inc(cast_done, 1)

            def take_zt(source, sweeps, products, width):
                act.wait_ge(step_done, Q * sweeps)
                wait(act, prod_done, products)
                a.activation(zt[:, :, 0:width], source[:, :, 0:width], ACT.Copy).then_inc(zt_ready, 1)

            def x_high(dest, q, scale):
                a.activation(dest[:, bass.ds(2 * q, 2), 0, :], x32[:, bass.ds(2 * q, 2), :], ACT.Copy,
                             scale=scale).then_inc(hi_done, 1)

            def spread_row(c, cp, width):
                act.wait_ge(slb_spread, c + 1)
                a.activation(slb[:, cp, 0:width], PA[cp][:, 0, 0:width], ACT.Copy).then_inc(slb_ready, 1)

            def exponentials(c, cp, q, slot, width):
                if first(c) and first(q):
                    act.wait_ge(slb_ready, 1)
                    act.wait_ge(cols_dve, 1)
                for mi in range(2):
                    ins = a.activation(wf[:, slot, mi, 0:width], slb[:, cp, 0:width], ACT.Exp, scale=-0.99,
                                       bias=wbias[:, bass.ds(2 * q + mi, 1)])
                ins.then_inc(exp_done, 1)

            def cap(b0, b1):
                act.wait_ge(dot_done, 2 * b1)
                a.activation(wcap[:, b0:b1], nsr[:, b0:b1], ACT.Exp, scale=0.01, bias=kcol[:, 2:3]).then_inc(cols_act, 1)

            def layer0(k, kp, casts=2, more=0):
                start, width = targets0(k)

                def step(q, qp, last):
                    wait(act, adj_kept, Q * 2 * k + q + 1)
                    wait(act, step_done, Q * k + q - 1)
                    a.activation(ring[:, (kp + qp) % 2, :, 0:width],
                                 adj_t[:, bass.ds(2 * q, 2), bass.ds(start, width)], ACT.Copy).then_inc(tile0, 1)
                    if k == CH - 1 and not (isinstance(q, int) and (q < 2 or q > Q - 3)):
                        act.wait_ge(step_done, Q * k + q - 1)
                        x_high(xs, q - 2, XS)
                spots, mids = {0: lambda: None, 1: lambda: None}, {}
                if first(k):
                    spots[0] = lambda: [x_high(xs, q, mxc[:, 3:4]) for q in range(AHEAD, Q)]
                else:
                    mids[0] = lambda: take_zt(pairs[1 - kp], k, 4 * k - 6, NARROW if k == 1 else WIDE)
                if first(k):
                    spots[2] = lambda: cast(2, 0, 0)
                    mids[2] = lambda: cast(2, 0, 1)
                elif casts > 0:
                    spots[1] = lambda: cast(2 * k + 2, 0, 0)
                    spots[2] = lambda: cast(2 * k + 2, 0, 1, more)
                if casts > 1:
                    spots[4] = lambda: cast(2 * k + 3, 1, 0)
                    spots[5] = lambda: cast(2 * k + 3, 1, 1)
                if k == CH - 1:
                    act.wait_ge(x_done, NB - 8)
                    spots[1] = lambda: cap(GROUPS[0], GROUPS[1])
                    spots[4] = lambda: spread_row(0, 0, WIDE)
                    spots[5] = lambda: (exponentials(0, 0, 0, 1, WIDE), exponentials(0, 0, 1, 0, WIDE))
                sweep(act, step, spots, mids)

            act.wait_ge(prep_dve, 8)
            for done, upto, pair, s in ((0, 4, 0, 0), (4, 6, 0, 1), (6, 8, 1, 0), (8, AHEAD, 1, 1)):
                for q in range(done, upto):
                    x_high(xs, q, mxc[:, 3:4])
                cast(pair, pair, s)
            layer0(0, 0)
            act.wait_ge(prep_read, 1)
            layer0(1, 1)
            layer0(2, 0)
            layer0(3, 1)
            layer0(4, 0)
            layer0(5, 1, casts=1, more=16)
            act.wait_ge(prep_dve, 27)
            layer0(6, 0, casts=0)

            def adj_tiles(sw, sp_, c, width, spots, mids={}):
                def step(q, qp, last):
                    act.wait_ge(step_done, Q * sw + q - 1)
                    a.activation(ring[:, (sp_ + qp) % 2, :, 0:width],
                                 adj_t[:, bass.ds(2 * q, 2), bass.ds(c * WIDE, width)], ACT.Copy).then_inc(tile_z, 1)
                sweep(act, step, spots, mids)

            def tanh_gates(c):
                act.wait_ge(gate_pre, c + 1)
                a.activation(gate[:, :, :], gate[:, :, :], ACT.Tanh, scale=0.5).then_inc(gate_tanh, 1)

            def tanh_block(blk, b):
                act.wait_ge(p1c, blk + 2)
                a.activation(t1[:, b, :], t1[:, b, :], ACT.Tanh, scale=0.5).then_inc(th_done, 1)

            def take_z(c, width):
                act.wait_ge(z_done, Q * (c + 1))
                act.wait_ge(prod_done, NB + 4 * c)
                a.activation(zt[:, :, 0:width], PZ[:, :, 0:width], ACT.Copy).then_inc(zt_ready, 1)

            def take_ut(c, cp, width):
                act.wait_ge(step_done, Q * (SW1 + c + 1))
                act.wait_ge(prod_done, NB + 4 * c)
                a.activation(ut[:, :, 0:width], PA[cp][:, :, 0:width], ACT.Copy).then_inc(ut_ready, 1)

            def middle_blocks():
                take_zt(pairs[0], SW1, NB - 4, WIDE)
                act.wait_ge(x_done, NB - 4)
                x_high(xs, Q - 4, XS)
                x_high(xs, Q - 3, XS)

            def last_blocks():
                act.wait_ge(x_done, NB)
                act.wait_ge(step_done, Q * SW1)
                x_high(xs, Q - 2, XS)
                x_high(xs, Q - 1, XS)
                cap(GROUPS[2], GROUPS[3])
                a.activation(ccol[:, :], slc[:, :], ACT.Exp, scale=-0.01, bias=kcol[:, 3:4]).then_inc(cols_act, 1)

            def layer1(c, cp, width):
                slotted = (1 + cp) % 2
                mids = {}

                def high(q, slot):
                    act.wait_ge(masked, Q * c + q + 1)
                    if not (first(c) and isinstance(q, int) and q < 2):
                        act.wait_ge(step_done, Q * (SW1 + c) + q - 1)
                    a.activation(wr[:, slot, 0, :, 0:width], wf[:, slot, :, 0:width], ACT.Copy).then_inc(w_high, 1)

                def tiles(q, slot, early):
                    if early:
                        act.wait_ge(step_done, Q * SW1 + q - 1)
                    else:
                        act.wait_ge(z_done, Q * c + q - 1)
                    for mi in range(2):
                        ins = a.activation(ring[:, slot, mi, 0:width], adj_t[:, 2 * q + mi, bass.ds(c * WIDE, width)],
                                           ACT.Copy, accum_out=degp[:, bass.ds(c * NB + 2 * q + mi, 1)])
                    ins.then_inc(tile_z, 1)

                def step(q, qp, last):
                    slot = (slotted + qp) % 2
                    early = first(c) and isinstance(q, int) and q < 2
                    if not early:
                        act.wait_ge(w_low, Q * c + q - 1)
                        act.wait_ge(w_added, Q * c + q - 1)
                    if first(c) and isinstance(q, int) and 2 * q in GROUPS[1:]:
                        act.wait_ge(cols_dve, GROUPS.index(2 * q) + 1)
                    second = isinstance(q, int) and q == 1
                    if second:
                        high(0, 1 - slot)
                    if not early:
                        exponentials(c, cp, q, slot, width)
                    if not first(q) and not second:
                        high(q - 1, 1 - slot)
                    tiles(q, slot, early)
                    if isinstance(c, int) and c == CH - 2 and first(q):
                        act.wait_ge(x_done, NB + 2 * EARLY + 2)
                        x_high(xs2, 0, XS)

                def early_pair(j):
                    x_high(xs2, 2 * j + 1, XS)
                    x_high(xs2, 2 * j + 2, XS)

                if first(c):
                    mids = {0: middle_blocks}
                    spots = {0: lambda: None, 1: lambda: cap(GROUPS[1], GROUPS[2]), 5: last_blocks}
                else:
                    spots = {0: lambda: take_z(c - 1, WIDE), 1: lambda: (take_ut(c - 1, 1 - cp, WIDE), tanh_gates(c - 1))}
                    for b in range(3):
                        spots[b + 3] = lambda b=b: tanh_block(4 * (c - 1) + b, b)
                    if isinstance(c, int) and c == CH - 2:
                        take = spots[0]
                        spots[0] = lambda: (take(), early_pair(0))
                        for j in (1, 2):
                            spots[j + 2] = lambda j=j, old=spots[j + 2]: (old(), early_pair(j))
                if not (isinstance(c, int) and c == CH - 1):
                    nextw = NARROW if isinstance(c, int) and c == CH - 2 else WIDE
                    spots[5] = lambda old=spots.get(5, lambda: None): (old(), spread_row(c + 1, 1 - cp, nextw))
                if not first(c):
                    act.wait_ge(slb_ready, c + 1)
                sweep(act, step, spots, mids)
                high(Q - 1, slotted)
                if not first(c):
                    tanh_block(4 * (c - 1) + 3, 3)

            chunks(act, layer1)
            take_z(CH - 1, NARROW)
            take_ut(CH - 1, 0, NARROW)

            def later(first_q, end_q, blocks_done):
                act.wait_ge(x_done, blocks_done)
                for q in range(first_q, end_q):
                    x_high(xs, q, XS)

            def layer2(c, cp, width):
                mids = {}
                if first(c):
                    spots = {0: lambda: later(EARLY, Q - 3, 2 * NB - 6), 1: lambda: later(Q - 3, Q - 1, 2 * NB - 2),
                             2: lambda: tanh_gates(CH - 1),
                             3: lambda: (tanh_block(4 * (CH - 1), 0), tanh_block(4 * (CH - 1) + 1, 1)),
                             5: lambda: later(Q - 1, Q, 2 * NB)}
                else:
                    spots = {0: lambda: None}
                    mids = {0: lambda: take_zt(pairs[cp], SW2 + c, 2 * NB + 4 * (c - 1), WIDE)}
                adj_tiles(SW2 + c, (SW2 + cp) % 2, c, width, spots, mids)
            chunks(act, layer2)

            def layer3(c, cp, width):
                spots = {0: lambda: None}
                if first(c):
                    mids = {0: lambda: take_zt(pairs[1], SW3, 2 * NB + 4 * (CH - 1), NARROW)}
                else:
                    mids = {0: lambda: take_zt(pairs[1 - cp], SW3 + c, 3 * NB + 4 * (c - 1), WIDE)}
                act.wait_ge(diag_added, c + 1)
                adj_tiles(SW3 + c, (SW3 + cp) % 2, c, width, spots, mids)
            chunks(act, layer3)
            take_zt(pairs[0], SW3 + CH, 3 * NB + 4 * (CH - 1), NARROW)

        @block.tensor
        def _(pe):
            mm = nc.tensor.matmul
            pe.wait_ge(const_made, 12)

            def weights_first():
                pe.wait_ge(prep_dve, 16)
                for i in range(4):
                    mm(prod[:, i * P:(i + 1) * P], ones[:, :], t_diag[:, i * P:(i + 1) * P], start=True, stop=True)
                pe.wait_ge(w_loaded, 16 * 7)
                for k in range(2):
                    ins = nc.tensor.transpose(pairs[1][:, 0, k * P:(k + 1) * P], t_w32[:, k, :], idf[:, :])
                ins.then_inc(prep_pe, 1)

            def weights_second():
                pe.wait_ge(prep_dve, 18)
                for k in range(2):
                    mm(pairs[1][:, 1, k * D:(k + 1) * D], t_w31[:, k * P:(k + 1) * P], t_w32t, start=True, stop=True)
                mm(pairs[1][:, 0, D:2 * D], t_b31, t_w32t, start=True, stop=True).then_inc(prep_pe, 1)

            def quads(h, q, qp, hp):
                bank = (hp + qp) % 2
                wait(pe, adj_kept, Q * h + q - 1)
                for j in range(2):
                    for mi in range(2):
                        blockm = rawb[:, 2 * hp + j, bass.ds((2 * q + mi) * P, P)]
                        ins = nc.tensor.transpose(turned[:, bank, mi * NARROW + j * P:mi * NARROW + (j + 1) * P],
                                                  blockm, idb[:, :])
                ins.then_inc(quad_done, 1)

            def sum_step(bank, parts, q, slot, width, is_first, is_last, between=None):
                for mi in range(2):
                    if between and mi == 1:
                        between()
                    for f in range(2):
                        for part in range(2):
                            ins = mm(bank[:, f, 0:width], parts[:, 2 * q + mi, part, f * P:(f + 1) * P],
                                     ring[:, slot, mi, 0:width], start=(is_first and mi == 0 and part == 0),
                                     stop=(is_last and mi == 1 and part == 1), skip_group_check=True)
                ins.then_inc(step_done, 1)

            def spread(c, cp, width):
                pe.wait_ge(slq_made, c + 1)
                if first(c):
                    pe.wait_ge(adj_kept, Q * HALVES)
                for b in range(width // P):
                    ins = mm(PA[cp][:, 0, b * P:(b + 1) * P], slq[:, b:b + 1].broadcast_to([P, P]), idf[:, :],
                             start=True, stop=True)
                ins.then_inc(slb_spread, 1)

            def products(blk, zt_count, b0, w):
                pe.wait_ge(zt_ready, zt_count)
                wait(pe, y_done, blk)
                for b in range(2):
                    for k in range(2):
                        ins = mm(prodv[:, b, :], zt[:, k, (b0 + b) * P:(b0 + b + 1) * P], w[:, k, :],
                                 start=(k == 0), stop=(k == 1))
                    ins.then_inc(prod_done, 1)

            pe.wait_ge(cast_done, 2)

            def step0(q, qp, last):
                quads(0, q, qp, 0)
            sweep(pe, step0, {1: lambda: None})

            def layer0(k, kp, more=True):
                start, width = targets0(k)
                late = [False]
                wait(pe, zt_ready, k - 1)

                def step(q, qp, last):
                    units = two_quads(q, late[0])

                    def unit(i):
                        which, qq, qqp = units[i]
                        if which == 1 and first(qq):
                            pe.wait_ge(cast_done, 4 * k + 6)
                        quads(2 * k + 1 + which, qq, qqp, 1 - which)
                    if more:
                        unit(0)
                    if first(k):
                        pe.wait_ge(xs_ready, q + 1)
                    pe.wait_ge(tile0, Q * k + q + 1)
                    sum_step(pairs[kp], xs, q, (kp + qp) % 2, width, first(q), last,
                             (lambda: unit(1)) if more else None)
                if first(k):
                    spots = {4: weights_first, 5: weights_second}
                elif isinstance(k, int) and k == 1:
                    spots = {1: lambda: products(0, 1, 0, w02)}
                else:
                    spots = {1: lambda: products(4 * k - 6, k, 0, w02), 3: lambda: products(4 * k - 4, k, 2, w02)}
                if not more:
                    spots[2] = spots.pop(3)
                    spots[3] = lambda: spread(0, 0, WIDE)
                if more:
                    pe.wait_ge(cast_done, 4 * k + 4)
                sweep(pe, step, layer0_spots(late, spots))

            layer0(0, 0)
            pe.wait_ge(prep_read, 1)
            layer0(1, 1)
            with pe.Fori(1, 3) as i:
                layer0(2 * i, 0)
                layer0(2 * i + 1, 1)
            layer0(6, 0, more=False)

            def attention_products(blk, b):
                pe.wait_ge(p1c, blk + 1)
                for i, (src, w) in enumerate(((zt, wg), (ut, wsa))):
                    for k in range(2):
                        ins = mm(prodv[:, i, :], src[:, k, b * P:(b + 1) * P], w[:, k, :], start=(k == 0), stop=(k == 1))
                ins.then_inc(prod_done, 1)

            def gates_and_sums(c, cp, nblocks):
                pe.wait_ge(sums_made, c + 1)
                pe.wait_ge(small_read, c + 1)
                for b in range(nblocks):
                    mm(small[:, b:b + 1], wsum[:, cp, 0, b * P:(b + 1) * P], ones[:, 0:1], start=(b == 0), stop=False,
                       skip_group_check=True)
                pe.wait_ge(zt_ready, ZT1 + c + 1)
                for b in range(nblocks):
                    for k in range(2):
                        ins = mm(small[:, 8 + 2 * b:10 + 2 * b], zt[:, k, b * P:(b + 1) * P], wgate[:, k, :],
                                 start=False, stop=False, skip_group_check=True)
                ins.then_inc(gates_done, 1)

            def first_attention_products(c):
                pe.wait_ge(ut_ready, c + 1)
                attention_products(4 * c, 0)

            def layer1(c, cp, width):
                slotted = (1 + cp) % 2
                if first(c):
                    pe.wait_ge(zt_ready, ZT1 - 1)
                    spots = {0: lambda: products(NB - 4, ZT1, 0, w02), 1: lambda: products(NB - 2, ZT1, 2, w02)}
                else:
                    spots = {0: lambda: gates_and_sums(c - 1, 1 - cp, 4), 1: lambda: first_attention_products(c - 1)}
                    for b in range(1, 4):
                        spots[b + 1] = lambda b=b: attention_products(4 * (c - 1) + b, b)
                if not (isinstance(c, int) and c == CH - 1):
                    nextw = NARROW if isinstance(c, int) and c == CH - 2 else WIDE
                    spots[4] = lambda old=spots.get(4, lambda: None): (old(), spread(c + 1, 1 - cp, nextw))

                def step(q, qp, last):
                    slot = (slotted + qp) % 2
                    if first(c):
                        pe.wait_ge(xs_ready, Q + q + 1)
                    if first(q) and not first(c):
                        pe.wait_ge(zt_ready, ZT1 + c)
                    pe.wait_ge(tile_z, Q * c + q + 1)
                    for mi in range(2):
                        for f in range(2):
                            for part in range(2):
                                ins = mm(PZ[:, f, 0:width], xs[:, 2 * q + mi, part, f * P:(f + 1) * P],
                                         ring[:, slot, mi, 0:width], start=(first(q) and mi == 0 and part == 0),
                                         stop=(last and mi == 1 and part == 1), skip_group_check=True)
                    ins.then_inc(z_done, 1)
                    if first(q):
                        pe.wait_ge(slb_ready, c + 1)
                    pe.wait_ge(w_low, Q * c + q + 1)
                    for mi in range(2):
                        for f in range(2):
                            for i, (part, wpart) in enumerate(((1, 0), (0, 0), (0, 1))):
                                ins = mm(PA[cp][:, f, 0:width], xs[:, 2 * q + mi, part, f * P:(f + 1) * P],
                                         wr[:, slot, wpart, mi, 0:width], start=(first(q) and mi == 0 and i == 0),
                                         stop=(last and mi == 1 and i == 2), skip_group_check=True)
                    ins.then_inc(step_done, 1)
                sweep(pe, step, spots)

            chunks(pe, layer1)

            def layer2(c, cp, width):
                if first(c):
                    pe.wait_ge(zt_ready, ZT2)
                    spots = {0: lambda: gates_and_sums(CH - 1, 0, 2), 1: lambda: first_attention_products(CH - 1),
                             2: lambda: attention_products(4 * (CH - 1) + 1, 1)}
                else:
                    spots = {2: lambda: products(2 * NB + 4 * (c - 1), ZT2 + c, 0, w02),
                             4: lambda: products(2 * NB + 4 * (c - 1) + 2, ZT2 + c, 2, w02)}
                    pe.wait_ge(ut_ready, CH)
                    pe.wait_ge(zt_ready, ZT2 + c - 1)

                def step(q, qp, last):
                    if first(c):
                        pe.wait_ge(xs_ready, 2 * Q + q + 1)
                    pe.wait_ge(tile_z, Q * (CH + c) + q + 1)
                    own = xs2 if early[0] else xs
                    sum_step(pairs[1 - cp], own, q, (SW2 + cp + qp) % 2, width, first(q), last)
                early = [True]

                def past_early(old=spots.get(EARLY // 2, lambda: None)):
                    early[0] = False
                    old()
                spots[EARLY // 2] = past_early
                sweep(pe, step, spots)
                if first(c):
                    pe.wait_ge(w2_loaded, 32)
            chunks(pe, layer2)

            def r_sums(c, cp, nblocks):
                pe.wait_ge(q_made, c + 1)
                pe.wait_ge(q_read, c + 1)
                for b in range(nblocks):
                    ins = mm(small[:, b:b + 1], slb[:, cp, b * P:(b + 1) * P], ones[:, 0:1], start=(b == 0), stop=False,
                             skip_group_check=True)
                ins.then_inc(q_summed, 1)

            def layer3(c, cp, width):
                if first(c):
                    pe.wait_ge(small_read, CH + 1)
                    pe.wait_ge(ut_ready, CH)
                    pe.wait_ge(cols_pool, 7)
                    spots = {1: lambda: products(3 * NB - 2, ZT3, 0, w02)}
                else:
                    spots = {2: lambda: (r_sums(c - 1, 1 - cp, 4), products(3 * NB + 4 * (c - 1), ZT3 + c, 0, w3)),
                             4: lambda: products(3 * NB + 4 * (c - 1) + 2, ZT3 + c, 2, w3)}
                pe.wait_ge(zt_ready, ZT3 + c - 1)

                def step(q, qp, last):
                    if first(c):
                        pe.wait_ge(xs_ready, 3 * Q + q + 1)
                    pe.wait_ge(tile_z, Q * (2 * CH + c) + q + 1)
                    sum_step(pairs[cp], xs, q, (SW3 + cp + qp) % 2, width, first(q), last)
                sweep(pe, step, spots)
            chunks(pe, layer3)
            r_sums(CH - 1, 0, 2)
            products(4 * NB - 2, ZT3 + CH, 0, w3)

        @block.vector
        def _(dve):
            v = nc.vector
            made = [0]

            def prep(ins):
                made[0] += 1
                ins.then_inc(prep_dve, 1)
                dve.wait_ge(prep_dve, made[0])

            for i in range(3):
                dve.wait_ge(x_loaded[i], 16 if i < 2 else 48)
                b1 = CUTS[i + 1] + i // 2
                prep(v.tensor_reduce(mxp[:, i:i + 1], x32[:, CUTS[i]:b1, :].rearrange("p b d -> p (b d)"), AX.X, ALU.max,
                                     apply_absolute_value=True))
            prep(v.tensor_reduce(mxc[:, 0:1], mxp[:, :], AX.X, ALU.max))
            assert made[0] == 4
            dve.wait_ge(prep_pool, 1)
            prep(v.tensor_scalar(mxc[:, 1:2], mxc[:, 1:2], 2.0 ** -100, None, ALU.max))
            prep(v.tensor_scalar(mxc[:, 2:3].bitcast(I32), mxc[:, 1:2].bitcast(I32), EXPONENT, None, ALU.bitwise_and))
            prep(v.reciprocal(mxc[:, 3:4], mxc[:, 2:3]))
            prep(v.tensor_scalar(mxc[:, 3:4], mxc[:, 3:4], 2.0 ** 14, None, ALU.mult))
            assert made[0] == 8

            def weights_start():
                dve.wait_ge(w_loaded, 16 * 7)
                dve.wait_ge(const_made, 12)
                for side in range(2):
                    for k in range(2):
                        prep(v.scalar_tensor_tensor(out=t[:, 0, :], in0=wsa[:, k, :], scalar=1.0,
                                                    in1=t_asa[:, side * D:(side + 1) * D], op0=ALU.mult, op1=ALU.mult,
                                                    accum_out=vcol[:, 2 * side + k:2 * side + k + 1]))

            def weights_diagonals():
                for i in range(4):
                    prep(v.tensor_scalar(t_diag[:, i * P:(i + 1) * P], idf[:, :], vcol[:, i:i + 1], None, ALU.mult))
                assert made[0] == 16

            def weights_turned():
                dve.wait_ge(prep_pe, 1)
                prep(v.tensor_copy(t_w32t, pairs[1][:, 0, 0:D]))
                prep(v.tensor_scalar(t_b31, ones[:, :], b31c[:, :], None, ALU.mult))
                prep(v.tensor_copy(vrow[:, :, :], prodv))

            def weights_end():
                dve.wait_ge(prep_pe, 2)
                dve.wait_ge(late_loaded, 16 * 10)
                prep(v.tensor_copy(w3[:, :, :], pairs[1][:, 1, :].rearrange("p (k d) -> p k d", k=2)))
                prep(v.tensor_tensor(bias3[:, :], pairs[1][:, 0, D:2 * D], bias3[:, :], ALU.add))
                v.tensor_scalar(bias3[:, :], bias3[:, :], XS, None, ALU.mult)
                v.tensor_scalar(biasg[:, :], biasg[:, :], XS, None, ALU.mult).then_inc(prep_read, 1)
                prep(v.scalar_tensor_tensor(out=t[:, 0, :], in0=vrow[:, 1, :], scalar=1.0, in1=vrow[:, 1, :],
                                            op0=ALU.mult, op1=ALU.mult, accum_out=kcol[:, 0:1]))
                assert made[0] == 22

            def weights_scaled():
                prep(v.tensor_scalar(bias02[:, :], bias02[:, :], mxc[:, 3:4], None, ALU.mult))
                prep(v.tensor_scalar(mxc[:, 2:3], mxc[:, 2:3], 2.0 ** -14, None, ALU.mult))
                prep(v.tensor_scalar(sxcol[:, :], onecol[:, :], mxc[:, 2:3], None, ALU.mult))
                dve.wait_ge(prep_pool, 2)
                prep(v.tensor_scalar(kcol[:, 2:3], kcol[:, 1:2], -0.16, LN_WS, ALU.mult, ALU.add))
                prep(v.tensor_scalar(kcol[:, 3:4], kcol[:, 1:2], 0.16, -LN_WS, ALU.mult, ALU.add))
                assert made[0] == 27

            def x_low(dest, q, base, scale):
                two = bass.ds(2 * q, 2)
                dve.wait_ge(hi_done, base + q + 1)
                v.scalar_tensor_tensor(out=dest[:, two, 1, :], in0=x32[:, two, :], scalar=scale, in1=dest[:, two, 0, :],
                                       op0=ALU.mult, op1=ALU.subtract).then_inc(xs_ready, 1)

            def keep(h, q, qp, hp):
                dve.wait_ge(quad_done, Q * h + q + 1)
                v.tensor_copy(adj_t[:, bass.ds(2 * q, 2), bass.ds(h * NARROW, NARROW)],
                              turned[:, (hp + qp) % 2, 0:WIDE].rearrange("p (m n) -> p m n", m=2)).then_inc(adj_kept, 1)

            def variances(blk, n, place=0):
                for b in range(2):
                    wait_apart(dve, y_done, blk + b + 1)
                    v.bn_stats(st[:, b, :], x32[:, n + b, :]).then_inc(st_done, 1)
                for b in range(2):
                    wait_apart(dve, st_done, blk + b + 1)
                    v.bn_aggr(mv[:, 2 * place + b, :], st[:, b, :]).then_inc(mv_done, 1)

            def scale_rows(n, pair, place=0):
                dve.wait_ge(rstd_done, pair + 1)
                for b in range(2):
                    v.tensor_scalar(x32[:, n + b, :], x32[:, n + b, :], mv[:, 2 * place + b, 0:1],
                                    rstd[:, 2 * place + b:2 * place + b + 1],
                                    ALU.subtract, ALU.mult).then_inc(x_done, 1)

            def residual(blk, n, bias, col_a, col_b, affs=None):
                affs = blk if affs is None else affs
                dve.wait_ge(prod_done, blk + 2)
                for b in range(2):
                    v.scalar_tensor_tensor(out=prodv[:, b, :], in0=bias, scalar=col_a[:, bass.ds(n + b, 1)],
                                           in1=prodv[:, b, :], op0=ALU.mult, op1=ALU.add).then_inc(aff_done, 1)
                for b in range(2):
                    dve.wait_ge(aff_done, affs + b + 1)
                    v.scalar_tensor_tensor(out=x32[:, n + b, :], in0=prodv[:, b, :], scalar=col_b[:, bass.ds(n + b, 1)],
                                           in1=x32[:, n + b, :], op0=ALU.mult, op1=ALU.add).then_inc(y_done, 1)

            def finish(blk, n, pair, bias, col_a, col_b, affs=None):
                residual(blk, n, bias, col_a, col_b, affs)
                variances(blk, n)
                scale_rows(n, pair)

            def dots0(h):
                for b in range(2):
                    dve.wait_ge(x_done, 2 * h + b + 1)
                    for side, (sign, col) in enumerate(((1.0, slc), (-1.0, nsr))):
                        if b == 1:
                            dve.wait_ge(dot_done, 4 * h + side + 1)
                        v.scalar_tensor_tensor(out=t[:, side, :], in0=x32[:, 2 * h + b, :], scalar=sign,
                                               in1=vrow[:, side, :], op0=ALU.mult, op1=ALU.mult,
                                               accum_out=col[:, bass.ds(2 * h + b, 1)]).then_inc(dot_done, 1)

            def residual0(h):
                residual(2 * h, 2 * h, bias02[:, :], onecol, sxcol)

            def norm0(h):
                variances(2 * h, 2 * h)
                scale_rows(2 * h, h)

            def finish_spots(k):
                if isinstance(k, int) and k == 1:
                    return {2: lambda: residual0(0), 3: lambda: norm0(0)}
                one, two = 2 * k - 3, 2 * k - 2
                return {2: lambda: residual0(one), 3: lambda: scale_rows(2 * one, one), 4: lambda: residual0(two),
                        5: lambda: scale_rows(2 * two, two)}

            def finish_mids(k):
                if first(k):
                    return {3: weights_diagonals}
                if isinstance(k, int) and k == 1:
                    return {}
                one, two = 2 * k - 3, 2 * k - 2
                return {2: lambda: variances(2 * one, 2 * one), 3: lambda: dots0(one), 4: lambda: variances(2 * two, 2 * two)}

            def layer0(k, kp):
                late = [False]

                def step(q, qp, last):
                    for which, qq, qqp in two_quads(q, late[0]):
                        keep(2 * k + 1 + which, qq, qqp, 1 - which)
                    if first(k) and not (isinstance(q, int) and q >= Q - LOWS):
                        x_low(xs, q + LOWS, 0, mxc[:, 3:4])
                sweep(dve, step, layer0_spots(late, finish_spots(k) if not first(k) else
                      {3: weights_start, 4: weights_turned, 5: weights_end}), finish_mids(k))
                if not first(k):
                    dots0(2 * k - 2)
            with dve.Fori(0, LOWS) as q:
                x_low(xs, q, 0, mxc[:, 3:4])
            sweep(dve, lambda q, qp, last: keep(0, q, qp, 0), {})
            layer0(0, 0)
            weights_scaled()
            layer0(1, 1)
            with dve.Fori(1, 3) as i:
                layer0(2 * i, 0)
                layer0(2 * i + 1, 1)

            def scaled_parts(dest, col, q, his, base, ready):
                for mi in range(2):
                    v.tensor_scalar(dest[:, 2 * q + mi, 0, :], x32[:, 2 * q + mi, :], col[:, bass.ds(2 * q + mi, 1)], None,
                                    ALU.mult).then_inc(his, 1)
                for mi in range(2):
                    dve.wait_ge(his, base + 2 * q + mi + 1)
                    ins = v.scalar_tensor_tensor(out=dest[:, 2 * q + mi, 1, :], in0=x32[:, 2 * q + mi, :],
                                                 scalar=col[:, bass.ds(2 * q + mi, 1)],
                                                 in1=dest[:, 2 * q + mi, 0, :], op0=ALU.mult, op1=ALU.subtract)
                ins.then_inc(ready, 1)

            def stage_left(c, nblocks):
                wait(dve, slb_spread, c)
                v.tensor_copy(slq[:, 0:nblocks], slc[:, bass.ds(4 * c, nblocks)]).then_inc(slq_made, 1)

            dve.wait_ge(dot_done, 8)
            v.tensor_copy(slq[:, 0:4], slc[:, 0:4]).then_inc(slq_made, 1)

            def weight_bias(b0, b1):
                dve.wait_ge(dot_done, 2 * b1)
                v.tensor_scalar(wbias[:, b0:b1], nsr[:, b0:b1], kcol[:, 2:3], None, ALU.add).then_inc(cols_dve, 1)
            weight_bias(GROUPS[0], GROUPS[1])

            def final_step(q, qp, last):
                if not (isinstance(q, int) and (q < 2 or q > Q - 3)):
                    x_low(xs, q - 2, Q, XS)
            one, two = 2 * (CH - 1) - 3, 2 * (CH - 1) - 2
            sweep(dve, final_step, {1: lambda: None, 2: lambda: residual0(one), 3: lambda: residual0(two),
                                    4: lambda: dots0(one), 5: lambda: (scale_rows(2 * two, two), dots0(two))},
                  {2: lambda: norm0(one), 3: lambda: variances(2 * two, 2 * two)})
            weight_bias(GROUPS[1], GROUPS[2])

            def last_columns():
                weight_bias(GROUPS[2], GROUPS[3])
                v.memset(sm[:, :], 0.0).then_inc(p1c, 1)
                v.memset(den[:, :], 0.0).then_inc(small_read, 1)

            NCOL = 6

            def gate_dots(c, nblocks):
                dve.wait_ge(wx_loaded, 32)
                for b in range(nblocks):
                    for side in range(2):
                        if b > 0:
                            dve.wait_ge(xab_dots, 8 * c + 2 * b + side - 1)
                        v.scalar_tensor_tensor(out=t[:, side, :], in0=x32[:, 4 * c + b, :], scalar=1.0,
                                               in1=vrow[:, side, :], op0=ALU.mult, op1=ALU.mult,
                                               accum_out=xab[:, b, side:side + 1]).then_inc(xab_dots, 1)

            def attention_columns(c, nblocks):
                k = [0]

                def link(ins):
                    k[0] += 1
                    ins.then_inc(chunk_cols, 1)
                    dve.wait_ge(chunk_cols, NCOL * c + k[0])
                dve.wait_ge(cols_act, 4)
                dve.wait_ge(xab_dots, 8 * c + 2 * nblocks)
                n4 = slice(0, nblocks)
                link(v.tensor_tensor(xab[:, n4, :], xab[:, n4, :], bab[:, :].unsqueeze(1).broadcast_to([P, nblocks, 2]), ALU.add))
                dve.wait_ge(gates_done, c + 1)
                v.tensor_copy(sm[:, 0:nblocks], small[:, 0:nblocks])
                v.tensor_copy(sm[:, 4:4 + 2 * nblocks], small[:, 8:8 + 2 * nblocks]).then_inc(small_read, 1)
                dve.wait_ge(small_read, c + 2)
                v.scalar_tensor_tensor(out=gate[:, n4, :], in0=sm[:, 4:4 + 2 * nblocks].rearrange("p (b s) -> p b s", s=2),
                                       scalar=1.0 / XS, in1=xab[:, n4, :], op0=ALU.mult, op1=ALU.add).then_inc(gate_pre, 1)
                four = bass.ds(4 * c, nblocks)
                link(v.tensor_tensor(den[:, n4], sm[:, n4], ccol[:, four], ALU.mult))
                link(v.tensor_scalar(den[:, n4], den[:, n4], 1e-5, None, ALU.add))
                link(v.reciprocal(den[:, n4], den[:, n4]))
                link(v.tensor_tensor(den[:, n4], den[:, n4], ccol[:, four], ALU.mult))
                dve.wait_ge(gate_tanh, c + 1)
                link(v.tensor_scalar(coef[:, n4, :], gate[:, n4, :], 1.0, 0.5 / XS, ALU.add, ALU.mult))
                v.tensor_tensor(coef[:, n4, 0], coef[:, n4, 0], den[:, n4], ALU.mult).then_inc(q_col, 1)
                assert k[0] == NCOL
                dve.wait_ge(q_col, c + 1)

            def mix(blk, b):
                dve.wait_ge(prod_done, NB + blk + 1)
                v.tensor_tensor(t1[:, b, :], prodv[:, 0, :], biasg[:, :], ALU.add).then_inc(p1a, 1)
                dve.wait_ge(p1a, blk + 1)
                v.tensor_scalar(t1[:, b, :], t1[:, b, :], coef[:, b, 1:2], None, ALU.mult).then_inc(p1b, 1)
                dve.wait_ge(p1b, blk + 1)
                v.scalar_tensor_tensor(out=t1[:, b, :], in0=prodv[:, 1, :], scalar=coef[:, b, 0:1], in1=t1[:, b, :],
                                       op0=ALU.mult, op1=ALU.add).then_inc(p1c, 1)

            def residual1(c, b0):
                for b in range(b0, b0 + 2):
                    dve.wait_ge(th_done, 4 * c + b + 1)
                    v.scalar_tensor_tensor(out=x32[:, 4 * c + b, :], in0=t1[:, b, :], scalar=0.5,
                                           in1=x32[:, 4 * c + b, :], op0=ALU.mult, op1=ALU.add).then_inc(y_done, 1)
                variances(NB + 4 * c + b0, 4 * c + b0, b0 // 2)

            def scale1(c, b0):
                scale_rows(4 * c + b0, HALVES + 2 * c + b0 // 2, b0 // 2)

            def layer1(c, cp, width):
                slotted = (1 + cp) % 2

                def low(q, slot):
                    dve.wait_ge(w_high, Q * c + q + 1)
                    v.tensor_tensor(wr[:, slot, 1, :, 0:width], wf[:, slot, :, 0:width], wr[:, slot, 0, :, 0:width],
                                    ALU.subtract).then_inc(w_low, 1)

                def step(q, qp, last):
                    slot = (slotted + qp) % 2
                    second = isinstance(q, int) and q == 1
                    if second:
                        low(0, 1 - slot)
                    dve.wait_ge(exp_done, Q * c + q + 1)
                    if first(c) and isinstance(q, int) and 2 * q in GROUPS[1:]:
                        dve.wait_ge(cols_act, GROUPS.index(2 * q) + 1)
                    for mi in range(2):
                        ins = v.scalar_tensor_tensor(out=wf[:, slot, mi, 0:width], in0=wf[:, slot, mi, 0:width],
                                                     scalar=wcap[:, bass.ds(2 * q + mi, 1)],
                                                     in1=adj_t[:, 2 * q + mi, bass.ds(c * WIDE, width)],
                                                     op0=ALU.min, op1=ALU.mult)
                    ins.then_inc(masked, 1)
                    if not first(q) and not second:
                        low(q - 1, 1 - slot)
                    if isinstance(c, int) and c == CH - 2 and first(q):
                        x_low(xs2, 0, 2 * Q, XS)

                def early_pair(j):
                    x_low(xs2, 2 * j + 1, 2 * Q, XS)
                    x_low(xs2, 2 * j + 2, 2 * Q, XS)

                mids = {}
                if first(c):
                    dve.wait_ge(cols_act, 1)
                    h = HALVES - 1
                    spots = {1: lambda: (x_low(xs, Q - 4, Q, XS), x_low(xs, Q - 3, Q, XS), residual0(h - 1),
                                         variances(2 * h - 2, 2 * h - 2)),
                             2: lambda: (scale_rows(2 * h - 2, h - 1), dots0(h - 1)),
                             3: lambda: (stage_left(1, 4), residual0(h), variances(2 * h, 2 * h)),
                             4: lambda: (scale_rows(2 * h, h), dots0(h), last_columns()),
                             5: lambda: (x_low(xs, Q - 2, Q, XS), x_low(xs, Q - 1, Q, XS))}
                else:
                    spots = {0: lambda: None, 1: lambda: attention_columns(c - 1, 4)}
                    for b in range(4):
                        spots[b + 2] = lambda b=b: mix(4 * (c - 1) + b, b)
                    mids = {0: lambda: gate_dots(c - 1, 4), 5: lambda: residual1(c - 1, 0)}
                    if not (isinstance(c, int) and c == CH - 1):
                        nextb = 2 if isinstance(c, int) and c == CH - 2 else 4
                        spots[3] = lambda old=spots[3]: (old(), stage_left(c + 1, nextb))
                    if isinstance(c, int) and c == CH - 2:
                        spots[0] = lambda: early_pair(0)
                        for j in (1, 2):
                            spots[j + 2] = lambda j=j, old=spots[j + 2]: (old(), early_pair(j))
                sweep(dve, step, spots, mids)
                low(Q - 1, slotted)
                if not first(c):
                    residual1(c - 1, 2)
                    scale1(c - 1, 0)
                    scale1(c - 1, 2)
            chunks(dve, layer1)

            with dve.Fori(EARLY, Q - 1) as q:
                x_low(xs, q, 2 * Q, XS)
            gate_dots(CH - 1, 2)
            attention_columns(CH - 1, 2)
            mix(4 * (CH - 1), 0)
            mix(4 * (CH - 1) + 1, 1)
            residual1(CH - 1, 0)
            scale1(CH - 1, 0)
            x_low(xs, Q - 1, 2 * Q, XS)
            dve.wait_ge(tile_z, Q * CH)
            v.tensor_reduce(degb[:, :], degp[:, :].rearrange("p (c m) -> p m c", c=CH), AX.X, ALU.add).then_inc(cols_dve, 1)
            dve.wait_ge(cols_dve, 4)
            v.tensor_tensor(degb[:, :], degb[:, :], pad[:, :], ALU.add).then_inc(cols_dve, 1)
            dve.wait_ge(cols_dve, 5)
            v.reciprocal(degb[:, :], degb[:, :]).then_inc(cols_dve, 1)
            dve.wait_ge(cols_dve, 6)
            v.tensor_scalar(degb[:, :], degb[:, :], 1.0 / XS, None, ALU.mult).then_inc(cols_dve, 1)
            dve.wait_ge(cols_dve, 7)
            dve.wait_ge(w2_loaded, 32)
            v.tensor_scalar(bias02[:, :], bias02[:, :], XS, None, ALU.mult).then_inc(q_read, 1)
            dve.wait_ge(q_read, 1)

            QCUT = NB // 2

            def add_r(c, nth, width, m0, m1, cp=None):
                base = 0 if cp is None else QCUT * CH
                span = QCUT
                m_first = 0 if cp is None else QCUT
                chunk = bass.ds(c * WIDE, width)
                place = qacc[:, chunk] if cp is None else slb[:, cp, 0:width]
                for m in range(m0, m1):
                    before = base + span * nth + m - m_first
                    if m == 0:
                        ins = v.tensor_scalar(place, adj_t[:, m, chunk], r3[:, m:m + 1], None, ALU.mult)
                    else:
                        dve.wait_ge(q_added, before)
                        ins = v.scalar_tensor_tensor(out=place, in0=adj_t[:, m, chunk], scalar=r3[:, m:m + 1],
                                                     in1=qacc[:, chunk] if m == QCUT else place, op0=ALU.mult, op1=ALU.add)
                    ins.then_inc(q_added, 1)
                if m1 == NB:
                    dve.wait_ge(q_added, base + span * (nth + 1))
                    v.sem_inc(q_made, 1)

            def add_identity(c, nblocks):
                for b in range(nblocks):
                    blk = adj_t[:, bass.ds(4 * c + b, 1), bass.ds((4 * c + b) * P, P)]
                    ins = v.tensor_tensor(blk, blk, idb[:, :].unsqueeze(1), ALU.add)
                ins.then_inc(diag_added, 1)
                dve.wait_ge(diag_added, c + 1)

            def finish_two(L, c, b0, bias, col_a, col_b):
                finish(L * NB + 4 * c + b0, 4 * c + b0, L * HALVES + 2 * c + b0 // 2, bias, col_a, col_b,
                       (L - 1) * NB + 4 * c + b0)

            def parts3(q):
                scaled_parts(xs, r3x, q, hi_done, 3 * Q, xs_ready)

            def chunk2(c):
                finish_two(2, c, 0, bias02[:, :], rowsum, degb)
                add_identity(c, 4)
                add_r(c, c + 1, WIDE, 0, QCUT // 2)
                finish_two(2, c, 2, bias02[:, :], rowsum, degb)
                add_r(c, c + 1, WIDE, QCUT // 2, QCUT)

            dve.wait_ge(cols_pool, 7)
            add_r(CH - 2, 0, WIDE, 0, QCUT)
            with dve.Fori(0, 4) as c:
                chunk2(c)
            dve.wait_ge(x_done, 2 * NB + 16)
            with dve.Fori(0, EARLY // 2) as q:
                parts3(q)
            chunk2(4)
            with dve.Fori(EARLY // 2, EARLY) as q:
                parts3(q)
            finish_two(2, CH - 2, 0, bias02[:, :], rowsum, degb)
            finish_two(2, CH - 2, 2, bias02[:, :], rowsum, degb)
            dve.wait_ge(x_done, 3 * NB - 2)
            with dve.Fori(EARLY, Q - 1) as q:
                dve.wait_ge(step_done, Q * (SW3 - 1) + q + 1)
                parts3(q)
            finish(3 * NB - 2, NB - 2, 3 * HALVES - 1, bias02[:, :], rowsum, degb, 2 * NB - 2)
            dve.wait_ge(x_done, 3 * NB)
            dve.wait_ge(step_done, Q * SW3)
            parts3(Q - 1)

            add_identity(CH - 2, 4)
            add_identity(CH - 1, 2)
            add_r(CH - 1, CH - 1, NARROW, 0, QCUT)
            add_r(0, 0, WIDE, QCUT, NB, 0)

            def q_column(c, nblocks):
                dve.wait_ge(q_summed, c + 1)
                v.tensor_copy(qcol[:, bass.ds(4 * c, nblocks)], small[:, 0:nblocks]).then_inc(q_read, 1)
                dve.wait_ge(q_read, c + 2)

            def chunk3(c, cp):
                q_column(c, 4)
                finish_two(3, c, 0, bias3[:, :], qcol, r3b)
                add_r(c + 1, c + 1, WIDE, QCUT, QCUT + QCUT // 2, 1 - cp)
                finish_two(3, c, 2, bias3[:, :], qcol, r3b)
                add_r(c + 1, c + 1, WIDE, QCUT + QCUT // 2, NB, 1 - cp)

            with dve.Fori(0, 2) as i:
                chunk3(2 * i, 0)
                chunk3(2 * i + 1, 1)
            chunk3(4, 0)
            add_r(CH - 1, CH - 1, NARROW, QCUT, NB, 0)
            q_column(CH - 2, 4)
            finish_two(3, CH - 2, 0, bias3[:, :], qcol, r3b)
            finish_two(3, CH - 2, 2, bias3[:, :], qcol, r3b)
            q_column(CH - 1, 2)
            finish(4 * NB - 2, NB - 2, 4 * HALVES - 1, bias3[:, :], qcol, r3b, 3 * NB - 2)


_INS = ['x', 'adj', 'L0_gnn_W', 'L0_gnn_b', 'L1_gnn_W_sa', 'L1_gnn_a_sa', 'L1_gnn_W_gcnb', 'L1_gnn_b_gcnb',
        'L1_gnn_Wa', 'L1_gnn_ba', 'L1_gnn_Wb', 'L1_gnn_bb', 'L2_gnn_W', 'L2_gnn_b',
        'L3_gnn_W1', 'L3_gnn_b1', 'L3_gnn_W2', 'L3_gnn_b2']


def kernel(**inputs):
    import numpy as _np
    import concourse.bacc as _bacc
    from concourse import mybir as _mybir
    from concourse.bass_utils import run_bass_kernel_spmd as _run

    nc = _bacc.Bacc("TRN2", target_bir_lowering=False, num_devices=1, dynamic_dma_scratch_size=256)
    arrays, args = {}, []
    for name in _INS:
        a = _np.ascontiguousarray(inputs[name])
        arrays[f"in_{name}_dram"] = a
        args.append(nc.dram_tensor(f"in_{name}_dram", a.shape, _mybir.dt.from_np(a.dtype), kind="ExternalInput").ap())
    shape = tuple(inputs['x'].shape)
    args.append(nc.dram_tensor("out_0_dram", shape, _mybir.dt.float32, kind="ExternalOutput").ap())
    four_graph_layers(nc, *args)
    r = _run(nc, [arrays], core_ids=[0])
    return r.results[0]["out_0_dram"]
```
